# Optimizing a Trainium2 kernel written in Bass

```python
import numpy as np
import jax
import jax.numpy as jnp

def _softmax(x, axis=-1):
    return jax.nn.softmax(x, axis=axis)
def _gelu(x):
    return jax.nn.gelu(x, approximate=True)
def _silu(x):
    return jax.nn.silu(x)
def _sigmoid(x):
    return jax.nn.sigmoid(x)
def _layernorm(x, axis=-1, eps=1e-5):
    m = jnp.mean(x, axis=axis, keepdims=True)
    v = jnp.var(x, axis=axis, keepdims=True)
    return (x - m) / jnp.sqrt(v + eps)
def _scatter_add(tgt, idx, src, axis=0):
    return tgt.at[idx].add(src)
def _segment_sum(src, seg, n):
    return jax.ops.segment_sum(src, seg, n)

kernel_name = 'mk_adj_preln_d4_adj_256_886190'

def setup_inputs(seed: int = 0):
    np.random.seed(seed)
    _w = jnp.asarray
    def _rec_inputs():
        import jax
        import jax.numpy as jnp
        _gk = jax.random.key(seed)
        x = -0.0005207 + 1.001 * jax.random.normal(jax.random.fold_in(_gk, 1), (4096, 256), jnp.float32)
        _a = jax.random.bernoulli(jax.random.fold_in(_gk, 2), 0.0078125, (4096, 4096))
        adj = _a.astype(jnp.int32)
        return x, adj
    x, adj = _rec_inputs()
    def _L0_gnn_setup():
        import jax, jax.numpy as jnp
        import numpy as np
        N, FEAT = (8192, 256)
        NEG_SLOPE = 0.2
        MASK_VAL = jnp.float32(-9000000000000000.0)
        key = jax.random.key(seed)
        k1, k2, k3 = jax.random.split(key, 3)
        h = jax.random.normal(k1, (N, FEAT), dtype=jnp.float32)
        adj = jax.random.randint(k2, (N, N), 0, 2, dtype=jnp.int32)
        a = jax.random.normal(k3, (2 * FEAT, 1), dtype=jnp.float32) * 0.1
        return {'h': h, 'adj': adj, 'a': a}
    _L0_gnn_all = _L0_gnn_setup()
    _L0_gnn_in = {k: v for k, v in _L0_gnn_all.items() if k in ('a', )}
    del _L0_gnn_all

    def _L1_gnn_setup():
        import jax, jax.numpy as jnp
        import numpy as np
        N = 4096
        F = 256
        D = 64
        H = 4
        ALPHA = 0.2
        NEG = jnp.float32(-9000000000000000.0)

        def _gat_layer(x, adj, W, a):
            h = jnp.einsum('nf,hfd->hnd', x, W)
            f1 = jnp.einsum('hnd,hd->hn', h, a[:, :D])
            f2 = jnp.einsum('hnd,hd->hn', h, a[:, D:])
            e = jax.nn.leaky_relu(f1[:, :, None] + f2[:, None, :], ALPHA)
            e = jnp.where(adj[None, :, :] > 0, e, NEG)
            att = jax.nn.softmax(e, axis=-1)
            out = jax.nn.elu(jnp.einsum('hnm,hmd->hnd', att, h))
            n = x.shape[0]
            return out.transpose(1, 0, 2).reshape(n, -1)
        key = jax.random.key(seed)
        ks = jax.random.split(key, 6)
        x = jax.random.normal(ks[0], (N, F), jnp.float32)
        adj = jax.random.randint(ks[1], (N, N), 0, 2, jnp.int32)
        W1 = jax.random.normal(ks[2], (H, F, D), jnp.float32) * (1.414 / F ** 0.5)
        a1 = jax.random.normal(ks[3], (H, 2 * D), jnp.float32) * 0.1
        W2 = jax.random.normal(ks[4], (H, H * D, D), jnp.float32) * (1.414 / (H * D) ** 0.5)
        a2 = jax.random.normal(ks[5], (H, 2 * D), jnp.float32) * 0.1
        t = jnp.zeros((), jnp.float32)
        return {'t': t, 'x': x, 'adj': adj, 'W1': W1, 'a1': a1, 'W2': W2, 'a2': a2}
    _L1_gnn_all = _L1_gnn_setup()
    _L1_gnn_in = {k: v for k, v in _L1_gnn_all.items() if k in ('t', 'W1', 'a1', 'W2', 'a2', )}
    del _L1_gnn_all

    def _L2_gnn_setup():
        import jax, jax.numpy as jnp
        import numpy as np
        N, IN_C, OUT_C, H, CF = (4096, 256, 256, 8, 6)
        D = OUT_C // H
        key = jax.random.key(seed)
        ks = jax.random.split(key, 8)
        x = jax.random.normal(ks[0], (N, IN_C), dtype=jnp.float32)
        positions = jax.random.normal(ks[1], (N, 3), dtype=jnp.float32)
        curv_feats = jax.random.normal(ks[2], (N, CF), dtype=jnp.float32)
        adj = jax.random.randint(ks[3], (N, N), 0, 2, dtype=jnp.int32)
        W = jax.random.normal(ks[4], (OUT_C, IN_C), dtype=jnp.float32) * 0.05
        a_l = jax.random.normal(ks[5], (H, D), dtype=jnp.float32) * 0.1
        a_r = jax.random.normal(ks[6], (H, D), dtype=jnp.float32) * 0.1
        Wc = jax.random.normal(ks[7], (H, CF), dtype=jnp.float32) * 0.1
        gate = jnp.asarray(0.1, dtype=jnp.float32)
        return {'x': x, 'positions': positions, 'curv_feats': curv_feats, 'adj': adj, 'W': W, 'a_l': a_l, 'a_r': a_r, 'Wc': Wc, 'gate': gate}
    _L2_gnn_all = _L2_gnn_setup()
    _L2_gnn_in = {k: v for k, v in _L2_gnn_all.items() if k in ('positions', 'curv_feats', 'W', 'a_l', 'a_r', 'Wc', 'gate', )}
    del _L2_gnn_all

    def _L3_gnn_setup():
        import jax, jax.numpy as jnp
        import numpy as np
        N, IN_F, H, D = (4096, 256, 4, 64)
        NEG_SLOPE = 0.2
        key = jax.random.key(seed)
        ks = jax.random.split(key, 8)
        s_w = 1.0 / np.sqrt(H * D)
        s_u = 1.0
        return {'inputs': jax.random.normal(ks[0], (N, IN_F), jnp.float32), 'adj_mat': jax.random.randint(ks[1], (N, N), 0, 2, jnp.int32), 'weight': jax.random.normal(ks[2], (IN_F, H * D), jnp.float32) * s_w, 'weight_u': jax.random.normal(ks[3], (H, D, 1), jnp.float32) * s_u, 'weight_v': jax.random.normal(ks[4], (H, D, 1), jnp.float32) * s_u, 'bias': jax.random.normal(ks[5], (1, H * D), jnp.float32) * s_w, 'proj_w': jax.random.normal(ks[6], (H * D, IN_F), jnp.float32) * (1.0 / np.sqrt(IN_F)), 'proj_b': jax.random.normal(ks[7], (H * D,), jnp.float32) * (1.0 / np.sqrt(IN_F))}
    _L3_gnn_all = _L3_gnn_setup()
    _L3_gnn_in = {k: v for k, v in _L3_gnn_all.items() if k in ('weight', 'weight_u', 'weight_v', 'bias', 'proj_w', 'proj_b', )}
    del _L3_gnn_all

    return {
        "x": x,
        "adj": adj,
        "L0_gnn_a": _L0_gnn_in["a"],
        "L1_gnn_t": _L1_gnn_in["t"],
        "L1_gnn_W1": _L1_gnn_in["W1"],
        "L1_gnn_a1": _L1_gnn_in["a1"],
        "L1_gnn_W2": _L1_gnn_in["W2"],
        "L1_gnn_a2": _L1_gnn_in["a2"],
        "L2_gnn_positions": _L2_gnn_in["positions"],
        "L2_gnn_curv_feats": _L2_gnn_in["curv_feats"],
        "L2_gnn_W": _L2_gnn_in["W"],
        "L2_gnn_a_l": _L2_gnn_in["a_l"],
        "L2_gnn_a_r": _L2_gnn_in["a_r"],
        "L2_gnn_Wc": _L2_gnn_in["Wc"],
        "L2_gnn_gate": _L2_gnn_in["gate"],
        "L3_gnn_weight": _L3_gnn_in["weight"],
        "L3_gnn_weight_u": _L3_gnn_in["weight_u"],
        "L3_gnn_weight_v": _L3_gnn_in["weight_v"],
        "L3_gnn_bias": _L3_gnn_in["bias"],
        "L3_gnn_proj_w": _L3_gnn_in["proj_w"],
        "L3_gnn_proj_b": _L3_gnn_in["proj_b"],
    }

def reference(x, adj, L0_gnn_a, L1_gnn_t, L1_gnn_W1, L1_gnn_a1, L1_gnn_W2, L1_gnn_a2, L2_gnn_positions, L2_gnn_curv_feats, L2_gnn_W, L2_gnn_a_l, L2_gnn_a_r, L2_gnn_Wc, L2_gnn_gate, L3_gnn_weight, L3_gnn_weight_u, L3_gnn_weight_v, L3_gnn_bias, L3_gnn_proj_w, L3_gnn_proj_b):
    import jax
    import jax.numpy as jnp
    def _L0_gnn_ref(h, adj, a):
        import jax, jax.numpy as jnp
        import numpy as np
        N, FEAT = (8192, 256)
        NEG_SLOPE = 0.2
        MASK_VAL = jnp.float32(-9000000000000000.0)
        f = h.shape[1]
        wh1 = h @ a[:f]
        wh2 = h @ a[f:]
        e = jax.nn.leaky_relu(wh1 + wh2.T, negative_slope=NEG_SLOPE)
        e = jnp.where(adj > 0, e, MASK_VAL)
        attention = jax.nn.softmax(e, axis=1)
        h_prime = attention @ h
        return h_prime

    def _L1_gnn_ref(t, x, adj, W1, a1, W2, a2):
        import jax, jax.numpy as jnp
        import numpy as np
        N = 4096
        F = 256
        D = 64
        H = 4
        ALPHA = 0.2
        NEG = jnp.float32(-9000000000000000.0)

        def _gat_layer(x, adj, W, a):
            h = jnp.einsum('nf,hfd->hnd', x, W)
            f1 = jnp.einsum('hnd,hd->hn', h, a[:, :D])
            f2 = jnp.einsum('hnd,hd->hn', h, a[:, D:])
            e = jax.nn.leaky_relu(f1[:, :, None] + f2[:, None, :], ALPHA)
            e = jnp.where(adj[None, :, :] > 0, e, NEG)
            att = jax.nn.softmax(e, axis=-1)
            out = jax.nn.elu(jnp.einsum('hnm,hmd->hnd', att, h))
            n = x.shape[0]
            return out.transpose(1, 0, 2).reshape(n, -1)
        h1 = _gat_layer(x, adj, W1, a1)
        return _gat_layer(h1, adj, W2, a2)

    def _L2_gnn_ref(x, positions, curv_feats, adj, W, a_l, a_r, Wc, gate):
        import jax, jax.numpy as jnp
        import numpy as np
        N, IN_C, OUT_C, H, CF = (4096, 256, 256, 8, 6)
        D = OUT_C // H
        n = x.shape[0]
        h = (x @ W.T).reshape(n, H, D)
        e_l = jnp.einsum('nhd,hd->nh', h, a_l)
        e_r = jnp.einsum('nhd,hd->nh', h, a_r)
        logits = jax.nn.leaky_relu(e_l[:, None, :] + e_r[None, :, :], negative_slope=0.2)
        curv_pair = jnp.abs(curv_feats[:, None, :] - curv_feats[None, :, :])
        curv_bias = jnp.einsum('ijf,hf->ijh', curv_pair, Wc)
        logits = logits + gate * curv_bias
        mask = (adj > 0)[:, :, None]
        logits = jnp.where(mask, logits, jnp.float32(-1000000000.0))
        attn = jax.nn.softmax(logits, axis=1)
        out = jnp.einsum('ijh,jhd->ihd', attn, h)
        return out.reshape(n, H * D)

    def _L3_gnn_ref(inputs, adj_mat, weight, weight_u, weight_v, bias, proj_w, proj_b):
        import jax, jax.numpy as jnp
        import numpy as np
        N, IN_F, H, D = (4096, 256, 4, 64)
        NEG_SLOPE = 0.2
        support = (inputs @ weight).reshape(-1, H, D).transpose(1, 0, 2)
        f1 = jnp.einsum('hnd,hd->hn', support, weight_u[..., 0])[:, None, :]
        f2 = jnp.einsum('hnd,hd->hn', support, weight_v[..., 0])[:, :, None]
        scores = jax.nn.leaky_relu(f1 + f2, NEG_SLOPE)
        masked = scores * adj_mat.astype(scores.dtype)
        mask = masked != 0
        neg_inf = jnp.asarray(-jnp.inf, masked.dtype)
        m = jnp.max(jnp.where(mask, masked, neg_inf), axis=2, keepdims=True)
        m = jnp.where(jnp.isfinite(m), m, jnp.zeros_like(m))
        e = jnp.where(mask, jnp.exp(masked - m), jnp.zeros_like(masked))
        denom = e.sum(axis=2, keepdims=True)
        attn = jnp.where(denom > 0, e / jnp.where(denom > 0, denom, 1.0), jnp.zeros_like(e))
        out = jnp.einsum('hnm,hmd->hnd', attn, support)
        out = out.transpose(1, 0, 2).reshape(-1, H * D)
        out = out + bias
        out = out + inputs @ proj_w.T + proj_b
        return out

    h = jnp.maximum(_layernorm(x, axis=-1), 0.0)
    x = x + _L0_gnn_ref(h, adj, L0_gnn_a)
    h = jnp.maximum(_layernorm(x, axis=-1), 0.0)
    x = x + _L1_gnn_ref(L1_gnn_t, h, adj, L1_gnn_W1, L1_gnn_a1, L1_gnn_W2, L1_gnn_a2)
    h = jnp.maximum(_layernorm(x, axis=-1), 0.0)
    x = x + _L2_gnn_ref(h, L2_gnn_positions, L2_gnn_curv_feats, adj, L2_gnn_W, L2_gnn_a_l, L2_gnn_a_r, L2_gnn_Wc, L2_gnn_gate)
    h = jnp.maximum(_layernorm(x, axis=-1), 0.0)
    x = x + _L3_gnn_ref(h, adj, L3_gnn_weight, L3_gnn_weight_u, L3_gnn_weight_v, L3_gnn_bias, L3_gnn_proj_w, L3_gnn_proj_b)
    return x


_drawn_inputs = setup_inputs


def setup_inputs(seed=0):
    import zlib

    import numpy as np

    out = dict(_drawn_inputs(seed))
    spreads = {}
    factors = {'L1_gnn_a2': 8.0,
     'L2_gnn_curv_feats': 8.0,
     'L2_gnn_a_l': 7.924,
     'L2_gnn_a_r': 3.445,
     'L2_gnn_Wc': 8.0}
    for name, (base, spread) in spreads.items():
        noise = np.random.default_rng([zlib.crc32(name.encode()), seed]).standard_normal(out[name].shape)
        drawn = base * np.exp(spread * noise) if base else spread * noise
        out[name] = jnp.asarray(drawn.astype(out[name].dtype))
    for name, factor in factors.items():
        out[name] = (out[name] * factor).astype(out[name].dtype)
    return out
```

```python
from contextlib import ExitStack

import concourse.bass as bass
from concourse import mybir

F32 = mybir.dt.float32
I32 = mybir.dt.int32
BF16 = mybir.dt.bfloat16
ALU = mybir.AluOpType
ACT = mybir.ActivationFunctionType
AX = mybir.AxisListType
RMAX = bass.bass_isa.ReduceOp.max

N = 4096
F = 256
P = 128
NB = N // P
KC = F // P
BANK = 512
EPS = 1e-5
SLOPE = 0.2
POS = 1.0 - SLOPE
CAP = 70.0
IT = 1024
NIT = N // IT
IB = IT // P
UN = 8
NF = 6
R = 16
GN = N // R
IT2 = BANK
NIT2 = N // IT2
G2 = IT2 // R
JP = 256
KD = NF * R
KM = KD + R + 1
BIG = 1e9
SHIFT = 60.0


def chained(eng, sem):
    count = [0]

    def run(ins):
        count[0] += 1
        ins.then_inc(sem, 1)
        eng.wait_ge(sem, count[0])
    return run


def prepare(nc, sem, ps, keep, layer):
    name, nh, d, src, norm = layer["name"], layer["nh"], layer["d"], layer["src"], layer["norm"]
    C = F + 2 * nh
    CA = C + nh * bool(layer.get("nonzero"))
    proj = layer.get("proj")
    x, mean_v, ident, ones = keep["x"], keep["mean_v"], keep["ident"], keep["ones"]
    s_w, s_vec = sem("weights_in"), sem("vectors_in")
    s_wcat, s_link = sem("weights_ready"), sem("prep_chain")
    s_st, s_var, s_std, s_rstd = sem("row_stats"), sem("variance"), sem("deviation"), sem("rstd")
    s_h, s_t, s_tc, s_p, s_hs = sem("rows"), sem("turned_psum"), sem("turned"), sem("projected"), sem("kept")
    s_pm, s_M, s_dq, s_q, s_aux = sem("part_max"), sem("max_all"), sem("shifted"), sem("q"), sem("aux_ready")
    s_vs, s_vm, s_fi, s_ft, s_fit = sem("value_sums"), sem("mean_psum"), sem("fi"), sem("fi_psum"), sem("fi_rows")
    s_out = sem("prep_out")
    pair = layer.get("pair")
    s_pc, s_cM, s_rt, s_rrow = sem("curv_part_max"), sem("curv_max"), sem("bound"), sem("bound_rows")
    FK = max(1, nh * NB // P)
    FR = min(P, nh * NB)
    with ExitStack() as ctx:
        def sb(what, shape):
            return ctx.enter_context(nc.sbuf_tensor(f"{name}_{what}", shape, F32))
        hs = sb("hs", [P, NB, CA])
        wcat = sb("wcat", [P, KC, C])
        vecs = sb("vecs", [P, 2, F])
        wtmp = sb("wtmp", [P, KC, F])
        rows = sb("rows", [P, 2, F])
        turned = sb("turned", [P, 2, F])
        st = sb("st", [P, NB, 6])
        sm = sb("sm", [P, 6, NB])
        pm = sb("pm", [P, nh])
        M = sb("M", [P, nh])
        cap = sb("cap", [P, nh])
        vsum = sb("vsum", [P, F])
        q = sb("q", [P, NB, nh])
        fi = sb("fi", [P, NB, nh])
        fit = sb("fit", [P, FK, P])
        if proj:
            wproj = sb("wproj", [P, KC, F])
            pbias = sb("pbias", [P, 2, F])
        if pair:
            curv = sb("curv", [P, NB, NF])
            cmax = sb("cmax", [P, 2, NF])
            gw = sb("gw", [P, nh, NF])
            gate = sb("gate", [P, 1])
            far = sb("far", [P, 2, NB * NF])
            prod = sb("prod", [P, NB, nh * NF])
            bound = sb("bound", [P, 3, NB * nh])
            boundt = sb("boundt", [P, FK, P])
        rstd, shift = sm[:, 4, :], sm[:, 5, :]
        block = ctx.enter_context(nc.Block())

        @block.sync
        def _(sp):
            sp.dma_start(wcat[:, :, 0:F], layer["w"].rearrange("(c p) n -> p c n", p=P)).then_inc(s_w, 16)
            if nh > 1:
                sp.dma_start(vecs[:, 0, :], layer["jvec"].partition_broadcast(P)).then_inc(s_vec, 16)
                sp.dma_start(vecs[:, 1, :], layer["ivec"].partition_broadcast(P)).then_inc(s_vec, 16)
            else:
                for c in range(KC):
                    for col, vec in ((F, "jvec"), (F + 1, "ivec")):
                        sp.dma_start(wcat[:, c, col:col + 1],
                                     layer[vec][c * P:(c + 1) * P].unsqueeze(1)).then_inc(s_vec, 16)
            if proj:
                sp.dma_start(wproj[:], proj["w"].rearrange("(c p) n -> p c n", p=P)).then_inc(s_w, 16)
                for k in range(2):
                    sp.dma_start(pbias[:, k, :], proj["bias"][k].partition_broadcast(P)).then_inc(s_vec, 16)
            if pair:
                sp.dma_start(curv[:], pair["curv"].rearrange("(b p) f -> p b f", p=P)).then_inc(s_vec, 16)
                sp.dma_start(gw[:].rearrange("p h f -> p (h f)"),
                             pair["wc"].rearrange("h f -> (h f)").partition_broadcast(P)).then_inc(s_vec, 16)
                sp.dma_start(gate[:], pair["gate"].partition_broadcast(P)).then_inc(s_vec, 16)
            sp.wait_ge(s_aux, 1)
            sp.dma_start(layer["aux"].rearrange("b p c -> p b c"), hs[:]).then_inc(s_out, 16)
            sp.wait_ge(s_fit, FK)
            irow = layer["irow"].rearrange("b h n -> (b h) n")
            for k in range(FK):
                sp.dma_start(irow[k * FR:(k + 1) * FR, :], fit[0:FR, k, :]).then_inc(s_out, 16)
            if pair:
                sp.wait_ge(s_rrow, FK)
                brow = pair["brow"].rearrange("b h n -> (b h) n")
                for k in range(FK):
                    sp.dma_start(brow[k * P:(k + 1) * P, :], boundt[:, k, :]).then_inc(s_out, 16)
                sp.wait_ge(s_out, 16 + 32 * FK)
            else:
                sp.wait_ge(s_out, 16 + 16 * FK)

        @block.gpsimd
        def _(pool):
            pool.wait_ge(s_pm, 1)
            pool.partition_all_reduce(M[:], pm[:], P, RMAX).then_inc(s_M, 1)
            if pair:
                pool.wait_ge(s_pc, 1)
                pool.partition_all_reduce(cmax[:], cmax[:], P, RMAX).then_inc(s_cM, 1)

        @block.scalar
        def _(act):
            if norm:
                act.wait_ge(s_var, 1)
                act.activation(sm[:, 3, :], sm[:, 2, :], ACT.Sqrt).then_inc(s_std, 1)
                act.wait_ge(s_rstd, 1)
            with act.Fori(0, NB // 2) as t:
                for k in range(2):
                    b = t * 2 + k
                    act.wait_ge(s_t, b + 1)
                    row = src[:, bass.ds(b, 1), :].rearrange("p a c -> p (a c)")
                    if norm:
                        act.activation(rows[:, k, :], row, ACT.Relu, bias=shift[:, bass.ds(b, 1)],
                                       scale=rstd[:, bass.ds(b, 1)]).then_inc(s_h, 1)
                    else:
                        act.copy(rows[:, k, :], row).then_inc(s_h, 1)
            act.wait_ge(s_dq, 1)
            act.activation(q[:], q[:], ACT.Exp, scale=SLOPE).then_inc(s_q, 1)

        @block.tensor
        def _(pe):
            pe.sem_inc(s_t, 2)
            pe.sem_inc(s_p, 2)
            pe.wait_ge(s_w, 32 if proj else 16)
            pe.wait_ge(s_wcat, 1)
            with pe.Fori(0, NB // 2) as t:
                for k in range(2):
                    b = t * 2 + k
                    pe.wait_ge(s_h, b + 1)
                    for c in range(KC):
                        ins = pe.transpose(ps[:, k, c * P:(c + 1) * P], rows[:, k, c * P:(c + 1) * P], ident[:])
                    ins.then_inc(s_t, 1)
                    pe.wait_ge(s_tc, b + 1)
                    pe.wait_ge(s_hs, b + 1)
                    for c in range(KC):
                        ins = pe.matmul(ps[:, 2 + k, 0:C], turned[:, k, c * P:(c + 1) * P], wcat[:, c, :],
                                        start=c == 0, stop=c == KC - 1)
                    if proj:
                        for c in range(KC):
                            ins = pe.matmul(ps[:, 4 + k, 0:F], turned[:, k, c * P:(c + 1) * P], wproj[:, c, :],
                                            start=c == 0, stop=c == KC - 1)
                    ins.then_inc(s_p, 1)
            pe.wait_ge(s_vs, 1)
            pe.matmul(ps[:, 6, 0:F], ones[:], vsum[:], start=True, stop=True).then_inc(s_vm, 1)
            pe.wait_ge(s_fi, 1)
            flat = fi[:].rearrange("p b h -> p (b h)")
            for k in range(FK):
                pe.transpose(ps[0:FR, 7, k * P:(k + 1) * P], flat[:, k * FR:(k + 1) * FR], ident[:]).then_inc(s_ft, 1)
            if pair:
                pe.wait_ge(s_rt, 1)
                for k in range(FK):
                    pe.transpose(ps[:, 5, k * P:(k + 1) * P], bound[:, 0, k * P:(k + 1) * P], ident[:]).then_inc(s_ft, 1)

        @block.vector
        def _(dve):
            link = chained(dve, s_link)
            dve.sem_inc(s_hs, 2)
            if nh > 1:
                dve.wait_ge(s_w, 16)
                dve.wait_ge(s_vec, 64 if proj else 80 if pair else 32)
                for k in range(2):
                    link(dve.tensor_tensor(wtmp[:], wcat[:, :, 0:F],
                                           vecs[:, k, :].unsqueeze(1).broadcast_to([P, KC, F]), ALU.mult))
                    link(dve.tensor_reduce(wcat[:, :, F + k * nh:F + (k + 1) * nh],
                                           wtmp[:].rearrange("p c (h d) -> p c h d", d=d), AX.X, ALU.add))
                if proj:
                    link(dve.tensor_tensor(pbias[:, 0, :], pbias[:, 0, :], pbias[:, 1, :], ALU.add))
            else:
                dve.wait_ge(s_vec, 16 * 2 * KC)
            dve.nop().then_inc(s_wcat, 1)
            if norm:
                with dve.Fori(0, NB) as b:
                    dve.bn_stats(st[:, bass.ds(b, 1), :].rearrange("p a c -> p (a c)"),
                                 src[:, bass.ds(b, 1), :].rearrange("p a c -> p (a c)")).then_inc(s_st, 1)
                dve.wait_ge(s_st, NB)
                link(dve.tensor_tensor(sm[:, 0, :], st[:, :, 1], st[:, :, 4], ALU.add))
                link(dve.tensor_tensor(sm[:, 1, :], st[:, :, 1], st[:, :, 4], ALU.subtract))
                link(dve.tensor_tensor(sm[:, 1, :], sm[:, 1, :], sm[:, 1, :], ALU.mult))
                link(dve.tensor_tensor(sm[:, 2, :], st[:, :, 2], st[:, :, 5], ALU.add))
                link(dve.scalar_tensor_tensor(sm[:, 2, :], sm[:, 1, :], F / 4.0, sm[:, 2, :], ALU.mult, ALU.add))
                dve.tensor_scalar(sm[:, 2, :], sm[:, 2, :], 1.0 / F, EPS, ALU.mult, ALU.add).then_inc(s_var, 1)
                dve.wait_ge(s_std, 1)
                link(dve.reciprocal(rstd, sm[:, 3, :]))
                dve.scalar_tensor_tensor(shift, sm[:, 0, :], -0.5, rstd, ALU.mult, ALU.mult).then_inc(s_rstd, 1)
            with dve.Fori(0, NB // 2) as t:
                for k in range(2):
                    b = t * 2 + k
                    dve.wait_ge(s_t, b + 3)
                    dve.wait_ge(s_p, b + 1)
                    dve.tensor_copy(turned[:, k, :], ps[:, k, 0:F]).then_inc(s_tc, 1)
                    dve.wait_ge(s_p, b + 3)
                    if proj:
                        xb = x[:, bass.ds(b, 1), :].rearrange("p a c -> p (a c)")
                        dve.tensor_tensor(xb, xb, ps[:, 4 + k, 0:F], ALU.add)
                    dve.tensor_copy(hs[:, bass.ds(b, 1), 0:C].rearrange("p a c -> p (a c)"),
                                    ps[:, 2 + k, 0:C]).then_inc(s_hs, 1)
            dve.wait_ge(s_hs, NB + 2)
            if proj:
                link(dve.tensor_tensor(x[:], x[:], pbias[:, 0, :].unsqueeze(1).broadcast_to([P, NB, F]), ALU.add))
            dve.tensor_reduce(pm[:], hs[:, :, F:F + nh].rearrange("p b c -> p c b"), AX.X, ALU.max).then_inc(s_pm, 1)
            dve.tensor_reduce(vsum[:], hs[:, :, 0:F].rearrange("p b c -> p c b"), AX.X, ALU.add).then_inc(s_vs, 1)
            dve.wait_ge(s_M, 1)
            dve.tensor_tensor(q[:], hs[:, :, F:F + nh], M[:].unsqueeze(1).broadcast_to([P, NB, nh]),
                              ALU.subtract).then_inc(s_dq, 1)
            if pair:
                link(dve.memset(cap[:], 3e38))
            else:
                link(dve.tensor_scalar(cap[:], M[:], -POS, CAP, ALU.mult, ALU.add))
            dve.scalar_tensor_tensor(fi[:], hs[:, :, F + nh:C], POS, cap[:].unsqueeze(1).broadcast_to([P, NB, nh]),
                                     ALU.mult, ALU.min).then_inc(s_fi, 1)
            dve.wait_ge(s_vm, 1)
            link(dve.tensor_copy(mean_v[:], ps[:, 6, 0:F]))
            if pair:
                link(dve.tensor_scalar(far[:, 0, :], curv[:].rearrange("p b f -> p (b f)"), -1.0, None, ALU.mult))
                link(dve.tensor_reduce(cmax[:, 0, :], curv[:].rearrange("p b f -> p f b"), AX.X, ALU.max))
                dve.tensor_reduce(cmax[:, 1, :], far[:, 0, :].rearrange("p (b f) -> p f b", f=NF),
                                  AX.X, ALU.max).then_inc(s_pc, 1)
                link(dve.tensor_scalar(gw[:], gw[:], gate[:, 0:1], 0.0, ALU.mult, ALU.max))
                dve.wait_ge(s_cM, 1)
                f0 = far[:, 0, :].rearrange("p (b f) -> p b f", f=NF)
                f1 = far[:, 1, :].rearrange("p (b f) -> p b f", f=NF)
                link(dve.tensor_tensor(f0, f0, cmax[:, 0:1, :].broadcast_to([P, NB, NF]), ALU.add))
                link(dve.tensor_tensor(f1, curv[:], cmax[:, 1:2, :].broadcast_to([P, NB, NF]), ALU.add))
                link(dve.tensor_tensor(f0, f0, f1, ALU.max))
                pr = prod[:].rearrange("p b (h f) -> p b h f", f=NF)
                link(dve.tensor_tensor(pr, f0.unsqueeze(2).broadcast_to([P, NB, nh, NF]),
                                       gw[:].unsqueeze(1).broadcast_to([P, NB, nh, NF]), ALU.mult))
                b3 = [bound[:, k, :].rearrange("p (b h) -> p b h", h=nh) for k in range(3)]
                link(dve.tensor_reduce(b3[1], pr, AX.X, ALU.add))
                link(dve.tensor_tensor(b3[2], hs[:, :, F + nh:C], M[:].unsqueeze(1).broadcast_to([P, NB, nh]), ALU.add))
                link(dve.tensor_scalar(bound[:, 2, :], bound[:, 2, :], 0.0, -POS, ALU.max, ALU.mult))
                link(dve.tensor_tensor(bound[:, 0, :], bound[:, 2, :], bound[:, 1, :], ALU.subtract))
                link(dve.tensor_scalar(bound[:, 0, :], bound[:, 0, :], SHIFT, None, ALU.add))
                dve.nop().then_inc(s_rt, 1)
            dve.wait_ge(s_q, 1)
            link(dve.tensor_scalar(hs[:, :, F:F + nh], hs[:, :, F:F + nh], POS, None, ALU.mult))
            link(dve.tensor_copy(hs[:, :, F + nh:C], q[:]))
            if CA > C:
                link(dve.tensor_scalar(hs[:, :, C:CA], hs[:, :, F:F + nh], -1.0, None, ALU.mult))
            v = hs[:, :, 0:F].rearrange("p b (h d) -> p b h d", d=d)
            for h in range(nh):
                ins = dve.tensor_tensor(v[:, :, h, :], v[:, :, h, :], q[:, :, h:h + 1].broadcast_to([P, NB, d]), ALU.mult)
            ins.then_inc(s_aux, 1)
            dve.wait_ge(s_ft, FK)
            for k in range(FK):
                dve.tensor_copy(fit[0:FR, k, :], ps[0:FR, 7, k * P:(k + 1) * P]).then_inc(s_fit, 1)
            if pair:
                dve.wait_ge(s_ft, 2 * FK)
                for k in range(FK):
                    dve.tensor_copy(boundt[:, k, :], ps[:, 5, k * P:(k + 1) * P]).then_inc(s_rrow, 1)


def finish_rows(dve, ps, keep, layer, it, blocks, bank_sums, bank_outs, bufs, sems):
    nh, elu, dst = layer["nh"], layer["elu"], layer.get("dst")
    den, att, tmp = bufs
    s_link, s_ot, s_post, s_mn, s_e = sems
    TB = blocks // 2
    d = F // nh
    links = 4 + TB * (1 + 2 * bool(layer["mean"]) + elu * (2 if dst is None else 1))
    count = [0]

    def link(ins):
        count[0] += 1
        ins.then_inc(s_link, 1)
        dve.wait_ge(s_link, it * links + count[0])
    sums = ps[:, bank_sums:bank_sums + 2, :].rearrange("p a (m r) -> p (a m) r", r=32)[:, :, 0]
    if nh > 1:
        link(dve.tensor_copy(den[:, 0].rearrange("p b h -> p (b h)"), sums))
    else:
        link(dve.tensor_reduce(den[:, 0].rearrange("p b h -> p (b h)"), sums.rearrange("p (b g) -> p b g", g=4),
                               AX.X, ALU.add))
    link(dve.tensor_scalar(den[:, 1], den[:, 0], 0.0, None, ALU.is_equal))
    link(dve.tensor_tensor(den[:, 2], den[:, 0], den[:, 1], ALU.add))
    link(dve.reciprocal(den[:, 3], den[:, 2]))
    wide = [P, 2, nh, d]
    a4 = att[:].rearrange("p b (h d) -> p b h d", h=nh)
    t4 = tmp[:].rearrange("p b (h d) -> p b h d", h=nh)
    m4 = keep["mean_v"][:].rearrange("p (h d) -> p h d", h=nh).unsqueeze(1).broadcast_to(wide)
    for r in range(TB):
        dve.wait_ge(s_ot, it * TB + r + 1)
        o = ps[:, bank_outs + r % 2, :].rearrange("p (b h d) -> p b h d", b=2, h=nh)
        rec = den[:, 3, 2 * r:2 * r + 2, :].unsqueeze(3).broadcast_to(wide)
        dve.tensor_tensor(a4, o, rec, ALU.mult).then_inc(s_post, 1)
        if layer["mean"]:
            none = den[:, 1, 2 * r:2 * r + 2, :].unsqueeze(3).broadcast_to(wide)
            link(dve.tensor_tensor(t4, m4, none, ALU.mult))
        dve.wait_ge(s_post, it * TB + r + 3)
        if layer["mean"]:
            link(dve.tensor_tensor(att[:], att[:], tmp[:], ALU.add))
        rows = (dst if dst is not None else keep["x"])[:, bass.ds(it * blocks + 2 * r, 2), :]
        if elu:
            dve.tensor_scalar(tmp[:], att[:], 0.0, None, ALU.min).then_inc(s_mn, 1)
            link(dve.tensor_scalar(att[:], att[:], 0.0, -1.0, ALU.max, ALU.add))
            dve.wait_ge(s_e, it * TB + r + 1)
            if dst is None:
                link(dve.tensor_tensor(att[:], att[:], tmp[:], ALU.add))
                link(dve.tensor_tensor(rows, rows, att[:], ALU.add))
            else:
                link(dve.tensor_tensor(rows, att[:], tmp[:], ALU.add))
        else:
            link(dve.tensor_tensor(rows, rows, att[:], ALU.add))
    assert count[0] == links, (count[0], links)


def attend(nc, sem, ps, keep, layer, adj_t):
    name, nh, elu, dst = layer["name"], layer["nh"], layer["elu"], layer.get("dst")
    x, mean_v, ident, zeros = keep["x"], keep["mean_v"], keep["ident"], keep["zeros"]
    C = F + 2 * nh + nh * bool(layer.get("nonzero"))
    G = 1 if nh > 1 else 4
    RING = 4 if nh > 1 else 8
    CR = RING // G
    DEN = 4
    TB = IB // 2
    s_in = [sem(f"tile_in{k}") for k in range(RING)]
    s_fi, s_u, s_p, s_pv = sem("fi_in"), sem("exps"), sem("weights"), sem("contracted")
    s_acc, s_ev, s_dt, s_ot, s_post = sem("tile_done"), sem("evacuated"), sem("sums_turned"), sem("outs_turned"), sem("outs_used")
    s_link, s_mn, s_e = sem("post_chain"), sem("negatives"), sem("elu_exp")
    mask, nonzero = layer.get("mask"), layer.get("nonzero")
    s_ed = sem("edges")
    s_ri, s_rc, s_ro = sem("adj_rows_in"), sem("adj_rows_less_1"), sem("adj_rows_out")
    with ExitStack() as ctx:
        def sb(what, shape, dt=F32):
            return ctx.enter_context(nc.sbuf_tensor(f"{name}_att_{what}", shape, dt))
        fi = sb("fi", [P, nh, IT])
        adj = sb("adj", [P, RING, IT], I32)
        aux = sb("aux", [P, RING, C])
        u = sb("u", [P, 4, IT])
        w = sb("w", [P, 8, IT])
        ot = sb("ot", [P, 6, BANK])
        den = sb("den", [P, 4, IB, nh])
        att = sb("att", [P, 2, F])
        tmp = sb("tmp", [P, 2, F])
        if nonzero:
            edges = sb("edges", [P, nh, IT], BF16)
        if mask:
            arows = sb("arows", [P, N], I32)
        block = ctx.enter_context(nc.Block())

        @block.sync
        def _(sp):
            with sp.Fori(0, NIT) as it:
                if nonzero:
                    sp.wait_ge(s_p, it * (nh * NB) + 4)
                else:
                    sp.wait_ge(s_u, it * (nh * NB) + 1)
                for h in range(nh):
                    sp.dma_start(fi[:, h, :].rearrange("p (b n) -> p b n", n=P),
                                 layer["irow"][bass.ds(it * IB, IB), h, :].partition_broadcast(P)).then_inc(s_fi, 16)
                with sp.Fori(0, NB // UN) as t:
                    for k in range(UN):
                        j = t * UN + k
                        g = it * (NB // G) + t * (UN // G) + k // G
                        if mask and k == 0:
                            row = it * (NB // UN) + t
                            sp.wait_ge(s_ro, row * 16 + 16)
                            sp.dma_start(arows[:], mask["adj"][bass.ds(row * P + mask["first"] * P, P), :]
                                         ).then_inc(s_ri, 16)
                        sp.wait_ge(s_pv, g + 1)
                        sp.dma_start(adj[:, k % RING, :],
                                     adj_t[bass.ds(j * P, P), bass.ds(it * IT, IT)]).then_inc(s_in[k % RING], 16)
                        sp.dma_start(aux[:, k % RING, :],
                                     layer["aux"][bass.ds(j, 1), :, :].rearrange("a p c -> (a p) c")
                                     ).then_inc(s_in[k % RING], 16)

        @block.scalar
        def _(act):
            act.sem_inc(s_u, 1)
            if mask:
                act.sem_inc(s_ro, 16)
            with act.Fori(0, NIT) as it:
                act.wait_ge(s_fi, it * (16 * nh) + 16 * nh)
                with act.Fori(0, NB // UN) as t:
                    for k in range(UN):
                        act.wait_ge(s_in[k % RING], (it * (NB // RING) + t * (UN // RING) + k // RING + 1) * 32)
                        for h in range(nh):
                            n = (it * NB + t * UN + k) * nh + h
                            act.wait_ge(s_p, n + 1)
                            act.activation(u[:, (k * nh + h) % 4, :], fi[:, h, :], ACT.Exp,
                                           bias=aux[:, k % RING, F + h:F + h + 1]).then_inc(s_u, 1)
                        if mask and k == 6:
                            row = it * (NB // UN) + t
                            act.wait_ge(s_rc, row + 1)
                            act.dma_start(mask["less_1"][bass.ds(row * P + mask["first"] * P, P), :],
                                          arows[:].bitcast(F32)).then_inc(s_ro, 16)
                act.wait_ge(s_acc, it + 1)
                for c in range(3):
                    act.copy(ot[:, c, :], ps[:, c, :]).then_inc(s_ev, 1)
                if elu:
                    for r in range(TB):
                        act.wait_ge(s_mn, it * TB + r + 1)
                        act.activation(tmp[:], tmp[:], ACT.Exp).then_inc(s_e, 1)
            if mask:
                act.wait_ge(s_ro, 16 + 16 * NIT * (NB // UN))

        @block.vector
        def _(dve):
            dve.sem_inc(s_p, 4)
            dve.sem_inc(s_post, 2)
            with dve.Fori(0, NIT) as it:
                with dve.Fori(0, NB // UN) as t:
                    for k in range(UN):
                        g = it * (NB // G) + t * (UN // G) + k // G
                        if mask and k == 4:
                            dve.wait_ge(s_ri, (it * (NB // UN) + t) * 16 + 16)
                            dve.tensor_scalar(arows[:].bitcast(F32), arows[:], -1.0, None, ALU.add).then_inc(s_rc, 1)
                        dve.wait_ge(s_pv, g + 1 + CR - 2)
                        for h in range(nh):
                            n = (it * NB + t * UN + k) * nh + h
                            dve.wait_ge(s_u, n + 2)
                            edge = adj[:, k % RING, :]
                            if nonzero:
                                edge = edges[:, h, :]
                                dve.scalar_tensor_tensor(edge, fi[:, h, :], aux[:, k % RING, C - nh + h:C - nh + h + 1],
                                                         adj[:, k % RING, :], ALU.not_equal, ALU.mult).then_inc(s_ed, 1)
                                dve.wait_ge(s_ed, n + 1)
                            dve.scalar_tensor_tensor(w[:, (k * nh + h) % 8, :], u[:, (k * nh + h) % 4, :], 1.0,
                                                     edge, ALU.max, ALU.mult).then_inc(s_p, 1)
                dve.wait_ge(s_acc, it + 1)
                for c in range(3, 6):
                    dve.tensor_copy(ot[:, c, :], ps[:, c, :]).then_inc(s_ev, 1)
                dve.wait_ge(s_dt, it + 1)
                finish_rows(dve, ps, keep, layer, it, IB, 6, 4, (den, att, tmp), (s_link, s_ot, s_post, s_mn, s_e))

        @block.tensor
        def _(pe):
            pe.sem_inc(s_pv, CR)
            with pe.Fori(0, NIT) as it:
                pe.wait_ge(s_post, it * TB + 2)
                for c in range(6):
                    pe.matmul(ps[:, c, :], zeros[:, 0:P], zeros[:], start=True, stop=False, skip_group_check=True)
                with pe.Fori(0, NB // UN) as t:
                    for k in range(UN):
                        n = (it * NB + t * UN + k) * nh
                        a = aux[:, k % RING, :]
                        if nh > 1:
                            for pair in range(nh // 2):
                                pe.wait_ge(s_p, n + 2 * pair + 6)
                                for c in range(2):
                                    for e in range(2):
                                        h = 2 * pair + e
                                        pe.matmul(ps[64 * e:64 * e + 64, 2 * pair + c, :], a[:, 64 * h:64 * h + 64],
                                                  w[:, (k * nh + h) % 8, c * BANK:(c + 1) * BANK],
                                                  start=False, stop=False, skip_group_check=True)
                        else:
                            pe.wait_ge(s_p, n + 5)
                            for half in range(2):
                                for c in range(2):
                                    pe.matmul(ps[:, 2 * half + c, :], a[:, half * P:(half + 1) * P],
                                              w[:, k, c * BANK:(c + 1) * BANK],
                                              start=False, stop=False, skip_group_check=True)
                        if (k + 1) % G == 0:
                            for c in range(2):
                                for e in range(4):
                                    kk, h = (k, e) if nh > 1 else (k - 3 + e, 0)
                                    q = aux[:, kk % RING, F + nh + h:F + nh + h + 1].broadcast_to([P, 32])
                                    ins = pe.matmul(ps[32 * e:32 * e + 32, DEN + c, :], q,
                                                    w[:, (kk * nh + h) % 8, c * BANK:(c + 1) * BANK],
                                                    start=False, stop=False, skip_group_check=True)
                            ins.then_inc(s_pv, 1)
                for c in range(6):
                    ins = pe.matmul(ps[:, c, :], zeros[:, 0:P], zeros[:], start=False, stop=True, skip_group_check=True)
                ins.then_inc(s_acc, 1)
                pe.wait_ge(s_ev, it * 6 + 6)
                for b in range(IB):
                    ins = pe.transpose(ps[:, 6 + b // 4, (b % 4) * P:(b % 4 + 1) * P],
                                       ot[:, DEN + b // 4, (b % 4) * P:(b % 4 + 1) * P], ident[:])
                ins.then_inc(s_dt, 1)
                for r in range(TB):
                    pe.wait_ge(s_post, it * TB + r + 1)
                    for e in range(2):
                        b = 2 * r + e
                        for half in range(2):
                            ins = pe.transpose(ps[:, 4 + r % 2, e * F + half * P:e * F + (half + 1) * P],
                                               ot[:, 2 * half + b // 4, (b % 4) * P:(b % 4 + 1) * P], ident[:])
                    ins.then_inc(s_ot, 1)


def attend_pairwise(nc, sem, ps, keep, layer):
    name, nh, pair = layer["name"], layer["nh"], layer["pair"]
    x, ident, zeros = keep["x"], keep["ident"], keep["zeros"]
    C = F + 2 * nh
    d = F // nh
    RING = 4
    TJ = 4
    NT = NB // TJ
    CG = 2 * BANK // P
    NCH = G2 // CG
    IB2 = IT2 // P
    OUT, SUM = 4, 6
    s_in = [sem(f"aux_in{k}") for k in range(RING)]
    s_m = [sem(f"edges_in{k}") for k in range(2)]
    s_c, s_c2, s_cc, s_fi, s_r, s_d, s_l = (sem("constants_in"), sem("coefficients"), sem("ones_set"), sem("fi_in"),
                                            sem("shift_in"), sem("differences"), sem("relus"))
    s_b, s_t, s_e, s_pv = sem("bias_psum"), sem("logits"), sem("weights"), sem("contracted")
    s_acc, s_ev, s_dt, s_ot, s_post, s_link = (sem("tile_done"), sem("evacuated"), sem("sums_turned"),
                                               sem("outs_turned"), sem("outs_used"), sem("post_chain"))
    s_copy, s_sub = sem("coefficient_chain"), sem("signed_differences")
    with ExitStack() as ctx:
        def sb(what, shape, dt=F32):
            return ctx.enter_context(nc.sbuf_tensor(f"{name}_att_{what}", shape, dt))
        diff = sb("diff", [P, 2, G2, JP])
        coef = sb("coef", [KM, G2, P])
        cj = sb("cj", [KD, N])
        ci = sb("ci", [KD, GN])
        gwr = sb("gwr", [KD, nh])
        gate = sb("gate", [KD, 1])
        fi = sb("fi", [P, nh, IT2])
        w = sb("w", [P, 2, nh, IT2])
        aux = sb("aux", [P, RING, C])
        ot = sb("ot", [P, 4, BANK])
        den = sb("den", [P, 4, IB2, nh])
        att = sb("att", [P, 2, F])
        tmp = sb("tmp", [P, 2, F])
        block = ctx.enter_context(nc.Block())

        @block.sync
        def _(sp):
            for f in range(NF):
                part = slice(f * R, (f + 1) * R)
                sp.dma_start(cj[part, :], pair["curv_t"][f, :].partition_broadcast(R)).then_inc(s_c, 16)
                sp.dma_start(gwr[part, :], pair["wc_t"][f, :].partition_broadcast(R)).then_inc(s_c, 16)
            sp.dma_start(ci[:], pair["curv_g"]).then_inc(s_c, 16)
            sp.dma_start(gate[:], pair["gate"].partition_broadcast(KD)).then_inc(s_c, 16)
            sp.dma_start(coef[0:KD, 0, :], pair["same_i"][0:KD, :]).then_inc(s_c, 16)
            for g in range(G2):
                sp.dma_start(coef[KD:KD + R, g, :], pair["same_i"][KD:KD + R, :]).then_inc(s_c, 16)
            sp.wait_ge(s_cc, 1)
            with sp.Fori(0, NIT2) as it:
                sp.wait_ge(s_b, it * (NB * NCH) + 16)
                for b in range(IB2):
                    sp.dma_start(coef[KM - 1:KM, b * 8:(b + 1) * 8, :].rearrange("p g (h n) -> p g h n", n=R),
                                 pair["brow"][bass.ds(it * IB2 + b, 1), :, :].rearrange("a h (g n) -> a g h n", n=R)
                                 ).then_inc(s_r, 16)
                sp.wait_ge(s_l, it * NB + 1)
                for h in range(nh):
                    sp.dma_start(fi[:, h, :].rearrange("p (b n) -> p b n", n=P),
                                 layer["irow"][bass.ds(it * IB2, IB2), h, :].partition_broadcast(P)).then_inc(s_fi, 16)
                with sp.Fori(0, NT) as t:
                    for k in range(TJ):
                        n = it * NB + t * TJ + k
                        if k % 2 == 0:
                            dp = it * (NB // 2) + t * (TJ // 2) + k // 2
                            sp.wait_ge(s_b, dp * (2 * NCH) + 2 * NCH)
                            sp.dma_start(diff[KD:KD + R, k // 2, :, :],
                                         pair["less_1"][bass.ds(it * IT2, IT2), bass.ds(t * (2 * JP) + (k // 2) * JP, JP)]
                                         .rearrange("(g i) j -> i g j", i=R)).then_inc(s_m[k // 2], 16)
                        sp.wait_ge(s_pv, n + 1)
                        sp.dma_start(aux[:, k, :], layer["aux"][bass.ds(t * TJ + k, 1), :, :]
                                     .rearrange("a p c -> (a p) c")).then_inc(s_in[k], 16)

        @block.scalar
        def _(act):
            act.sem_inc(s_l, 1)

            def relus(it, t, k):
                n = it * NB + t * TJ + k
                act.wait_ge(s_in[k % RING], (it * NT + t) * 16 + 16)
                act.wait_ge(s_pv, n + 3)
                for h in range(nh):
                    ins = act.activation(w[:, k % 2, h, :], fi[:, h, :], ACT.Relu, bias=aux[:, k % RING, F + h:F + h + 1])
                ins.then_inc(s_l, 1)

            def turn(it, t, last):
                for k in range(TJ):
                    if k + 1 < TJ:
                        relus(it, t, k + 1)
                    elif not last:
                        relus(it, t + 1, 0)
                    n = it * NB + t * TJ + k
                    act.wait_ge(s_t, n * NCH + NCH + 2)
                    flat = w[:, k % 2].rearrange("p h n -> p (h n)")
                    act.activation(flat, flat, ACT.Exp).then_inc(s_e, 1)

            with act.Fori(0, NIT2) as it:
                act.wait_ge(s_fi, it * (16 * nh) + 16 * nh)
                relus(it, 0, 0)
                with act.Fori(0, NT - 1) as t:
                    turn(it, t, False)
                turn(it, NT - 1, True)
                act.wait_ge(s_acc, it + 1)
                for c in range(2):
                    act.copy(ot[:, c, :], ps[:, OUT + c, :]).then_inc(s_ev, 1)

        @block.vector
        def _(dve):
            dve.sem_inc(s_t, 2)
            dve.sem_inc(s_post, 2)
            for e in range(2):
                ins = dve.memset(diff[KD:P, e], 1.0)
                ins.then_inc(s_copy, 1)
            dve.wait_ge(s_copy, 2)
            dve.nop().then_inc(s_cc, 1)
            dve.wait_ge(s_c, 16 * (2 * NF + 3 + G2))
            dve.tensor_scalar(gwr[:], gwr[:], gate[:, 0:1], None, ALU.mult).then_inc(s_copy, 1)
            dve.wait_ge(s_copy, 3)
            c0 = coef[0:KD, 0, :].rearrange("p (h n) -> p h n", n=R)
            dve.tensor_tensor(c0, c0, gwr[:].unsqueeze(2).broadcast_to([KD, nh, R]), ALU.mult).then_inc(s_copy, 1)
            dve.wait_ge(s_copy, 4)
            dve.tensor_copy(coef[0:KD, 1:G2, :], coef[0:KD, 0:1, :].broadcast_to([KD, G2 - 1, P])).then_inc(s_c2, 1)

            def differences(it, t, e, part):
                dp = it * (NB // 2) + t * (TJ // 2) + e
                if part == 0:
                    dve.wait_ge(s_b, dp * (2 * NCH) + 2 * NCH)
                for g in range(part * G2 // 2, (part + 1) * G2 // 2):
                    ins = dve.tensor_scalar(diff[0:KD, e, g, :], cj[:, bass.ds(t * (2 * JP) + e * JP, JP)],
                                            ci[:, bass.ds(it * G2 + g, 1)], None, ALU.subtract)
                ins.then_inc(s_sub, 1)
                dve.wait_ge(s_sub, dp * 2 + part + 1)
                half = diff[0:KD, e, part * G2 // 2:(part + 1) * G2 // 2, :].rearrange("p g j -> p (g j)").bitcast(I32)
                dve.tensor_scalar(half, half, 0x7fffffff, None, ALU.bitwise_and).then_inc(s_d, 1)

            def turn(it, t, last):
                for k in range(TJ):
                    n = it * NB + t * TJ + k
                    dve.wait_ge(s_l, n + 2)
                    for c in range(NCH):
                        dve.wait_ge(s_b, n * NCH + c + 1 + 16)
                        l = w[:, k % 2, :, c * P:(c + 1) * P].rearrange("p h (g i) -> p g h i", i=R)
                        bank = 2 * (c % 2)
                        b = ps[:, bank:bank + 2, :].rearrange("p a (g h i) -> p (a g) h i", h=nh, i=R)
                        dve.tensor_tensor(l, b, l, ALU.add).then_inc(s_t, 1)
                    if k < 2:
                        differences(it, t, 1, k % 2)
                    elif not last:
                        differences(it, t + 1, 0, k % 2)

            with dve.Fori(0, NIT2) as it:
                differences(it, 0, 0, 0)
                differences(it, 0, 0, 1)
                with dve.Fori(0, NT - 1) as t:
                    turn(it, t, False)
                turn(it, NT - 1, True)
                dve.wait_ge(s_acc, it + 1)
                for c in range(2, 4):
                    dve.tensor_copy(ot[:, c, :], ps[:, OUT + c, :]).then_inc(s_ev, 1)
                dve.wait_ge(s_dt, it + 1)
                finish_rows(dve, ps, keep, layer, it, IB2, 0, 2, (den, att, tmp), (s_link, s_ot, s_post, None, None))

        @block.tensor
        def _(pe):
            pe.sem_inc(s_b, 16)
            pe.sem_inc(s_pv, RING)
            pe.wait_ge(s_c2, 1)
            TB = IB2 // 2

            def bias(it, t, k):
                n = it * NB + t * TJ + k
                e = k // 2
                if k % 2 == 0:
                    dp = it * (NB // 2) + t * (TJ // 2) + e
                    pe.wait_ge(s_d, dp * 2 + 2)
                    pe.wait_ge(s_m[e], (it * NT + t) * 16 + 16)
                for c in range(NCH):
                    pe.wait_ge(s_t, n * NCH + c + 1)
                    for g in range(CG):
                        col = (g % 4) * P
                        ins = pe.matmul(ps[:, 2 * (c % 2) + g // 4, col:col + P],
                                        diff[0:KM, e, c * CG + g, (k % 2) * P:(k % 2 + 1) * P],
                                        coef[:, c * CG + g, :], start=True, stop=True)
                    ins.then_inc(s_b, 1)

            def contract(it, t, k):
                n = it * NB + t * TJ + k
                pe.wait_ge(s_e, n + 1)
                for s in range(nh // 4):
                    for q in range(4):
                        h = 4 * s + q
                        pe.matmul(ps[32 * q:32 * q + 32, OUT + s, :], aux[:, k, d * h:d * h + d], w[:, k % 2, h, :],
                                  start=False, stop=False, skip_group_check=True)
                for s in range(nh // 4):
                    for q in range(4):
                        h = 4 * s + q
                        ins = pe.matmul(ps[32 * q:32 * q + 32, SUM + s, :],
                                        aux[:, k, F + nh + h:F + nh + h + 1].broadcast_to([P, 32]), w[:, k % 2, h, :],
                                        start=False, stop=False, skip_group_check=True)
                ins.then_inc(s_pv, 1)

            def turn(it, t, last):
                for k in range(TJ):
                    if k + 1 < TJ:
                        bias(it, t, k + 1)
                    elif not last:
                        bias(it, t + 1, 0)
                    contract(it, t, k)

            with pe.Fori(0, NIT2) as it:
                for c in range(4):
                    pe.matmul(ps[:, OUT + c, :], zeros[:, 0:P], zeros[:], start=True, stop=False, skip_group_check=True)
                pe.wait_ge(s_r, it * (16 * IB2) + 16 * IB2)
                pe.wait_ge(s_post, it * TB + 2)
                bias(it, 0, 0)
                with pe.Fori(0, NT - 1) as t:
                    turn(it, t, False)
                turn(it, NT - 1, True)
                for c in range(4):
                    ins = pe.matmul(ps[:, OUT + c, :], zeros[:, 0:P], zeros[:], start=False, stop=True, skip_group_check=True)
                ins.then_inc(s_acc, 1)
                pe.wait_ge(s_ev, it * 4 + 4)
                for b in range(IB2):
                    for s in range(2):
                        m = b * 2 + s
                        ins = pe.transpose(ps[:, m // 4, (m % 4) * P:(m % 4 + 1) * P],
                                           ot[:, 2 + s, b * P:(b + 1) * P], ident[:])
                ins.then_inc(s_dt, 1)
                for r in range(TB):
                    pe.wait_ge(s_post, it * TB + r + 1)
                    for e in range(2):
                        b = 2 * r + e
                        for s in range(2):
                            ins = pe.transpose(ps[:, 2 + r % 2, e * F + s * P:e * F + (s + 1) * P],
                                               ot[:, s, b * P:(b + 1) * P], ident[:])
                    ins.then_inc(s_ot, 1)


def build(nc, a, out, layers):
    with ExitStack() as ctx:
        def sb(name, shape, dt=F32):
            return ctx.enter_context(nc.sbuf_tensor(name, shape, dt))

        def dram(name, shape, dt=F32):
            return nc.dram_tensor(name, shape, dt, kind="Internal").ap()

        def phase(f, prefix, *args):
            made = []

            def sem(name):
                made.append(nc.alloc_semaphore(name=f"{prefix}_{name}"))
                return made[-1]
            f(nc, sem, ps, keep, *args)
            nc.clear_and_free_semaphores(made)
            nc.all_engine_barrier()
        ps = ctx.enter_context(nc.psum_tensor("ps", [P, 8, BANK], F32))
        keep = {
            "x": sb("x", [P, NB, F]), "mean_v": sb("mean_v", [P, F]), "ident": sb("ident", [P, P]),
            "ones": sb("ones", [P, P]), "zeros": sb("zeros", [P, BANK], BF16),
        }
        x = keep["x"]
        s_x, s_c = ctx.enter_context(nc.semaphore("x_in")), ctx.enter_context(nc.semaphore("constants"))
        with nc.Block() as block:
            @block.sync
            def _(sp):
                sp.dma_start(x[:], a["x"].rearrange("(b p) f -> p b f", p=P)).then_inc(s_x, 16)
                sp.dma_start(keep["ident"][:], a["ident"]).then_inc(s_x, 16)
                sp.wait_ge(s_x, 32)

            @block.vector
            def _(dve):
                dve.memset(keep["ones"][:], 1.0 / N).then_inc(s_c, 1)
                dve.memset(keep["zeros"][:], 0.0).then_inc(s_c, 1)
                dve.wait_ge(s_c, 2)
        w1a, w1b = a["W1"], a["W2"]
        less_1 = dram("less_1", [N, N])
        if "0" in layers:
            l0 = dict(name="l0", nh=1, d=F, src=x, norm=True, w=a["eye"], jvec=a["a0"][F:2 * F, 0], ivec=a["a0"][0:F, 0],
                      aux=dram("aux0", [NB, P, F + 2]), irow=dram("irow0", [NB, 1, P]), elu=False, mean=True)
            phase(prepare, "p0", l0)
            phase(attend, "l0", l0, a["adj_t"])
        if "1" in layers:
            with nc.sbuf_tensor("h1", [P, NB, F], F32) as h1:
                for name, src, w, av, dst in (("l1a", x, w1a, a["a1"], h1), ("l1b", h1, w1b, a["a2"], None)):
                    l1 = dict(name=name, nh=4, d=64, src=src, norm=dst is not None, w=w, jvec=av[1], ivec=av[0],
                              aux=dram("aux" + name, [NB, P, F + 8]), irow=dram("irow" + name, [NB, 4, P]),
                              elu=True, mean=True, dst=dst,
                              mask={"adj": a["adj"], "less_1": less_1, "first": 0 if dst is not None else NB // 2})
                    phase(prepare, "p" + name, l1)
                    phase(attend, name, l1, a["adj_t"])
        if "2" in layers:
            l2 = dict(name="l2", nh=8, d=32, src=x, norm=True, w=a["w2"], jvec=a["ar2"], ivec=a["al2"],
                      aux=dram("aux2", [NB, P, F + 16]), irow=dram("irow2", [NB, 8, P]), elu=False, mean=True,
                      pair={"curv": a["curv"], "wc": a["wc"], "gate": a["gate"], "brow": dram("brow2", [NB, 8, P]),
                            "curv_t": a["curv_t"], "wc_t": a["wc_t"], "curv_g": a["curv_g"], "same_i": a["same_i"],
                            "less_1": less_1})
            phase(prepare, "p2", l2)
            phase(attend_pairwise, "l2", l2)
        if "3" in layers:
            l3 = dict(name="l3", nh=4, d=64, src=x, norm=True, w=a["w3"], jvec=a["u3"], ivec=a["v3"],
                      aux=dram("aux3", [NB, P, F + 12]), irow=dram("irow3", [NB, 4, P]),
                      elu=False, mean=False, nonzero=True, proj={"w": a["pw3"], "bias": [a["b3"], a["pb3"]]})
            phase(prepare, "p3", l3)
            phase(attend, "l3", l3, a["adj_t"])
        s_o = ctx.enter_context(nc.semaphore("out_written"))
        with nc.Block() as block:
            @block.sync
            def _(sp):
                sp.dma_start(out.rearrange("(b p) f -> p b f", p=P), x[:]).then_inc(s_o, 16)
                sp.wait_ge(s_o, 16)


LAYERS = "0123"


def kernel(**inputs):
    import numpy as _np
    import concourse.bacc as _bacc
    from concourse import mybir as _mybir
    from concourse.bass_utils import run_bass_kernel_spmd as _run

    i = {k: _np.asarray(v) for k, v in inputs.items()}
    heads = lambda w: w.transpose(1, 0, 2).reshape(F, F)
    halves = lambda v: v.reshape(4, 2, 64).transpose(1, 0, 2).reshape(2, F)
    same_i = _np.zeros((KD + R, 8, R), _np.float32)
    for r in range(R):
        same_i[r:KD:R, :, r] = 1.0
        same_i[KD + r, :, r] = BIG
    curv = i["L2_gnn_curv_feats"]
    put = {
        "adj": i["adj"], "w2": i["L2_gnn_W"].T, "al2": i["L2_gnn_a_l"].reshape(F), "ar2": i["L2_gnn_a_r"].reshape(F),
        "curv": curv, "curv_t": curv.T, "curv_g": curv.reshape(GN, R, NF).transpose(2, 1, 0).reshape(KD, GN),
        "wc": i["L2_gnn_Wc"], "wc_t": i["L2_gnn_Wc"].T, "gate": i["L2_gnn_gate"].reshape(1),
        "same_i": same_i.reshape(KD + R, P),
        "x": i["x"], "adj_t": i["adj"].T, "a0": i["L0_gnn_a"],
        "W1": heads(i["L1_gnn_W1"]), "a1": halves(i["L1_gnn_a1"]),
        "W2": heads(i["L1_gnn_W2"]), "a2": halves(i["L1_gnn_a2"]),
        "w3": i["L3_gnn_weight"], "u3": i["L3_gnn_weight_u"].reshape(F), "v3": i["L3_gnn_weight_v"].reshape(F),
        "b3": i["L3_gnn_bias"].reshape(F), "pb3": i["L3_gnn_proj_b"], "pw3": i["L3_gnn_proj_w"].T,
        "ident": _np.eye(P, dtype=_np.float32), "eye": _np.eye(F, dtype=_np.float32),
    }
    nc = _bacc.Bacc("TRN2", target_bir_lowering=False, num_devices=1)
    arrays, aps = {}, {}
    for name, v in put.items():
        v = _np.ascontiguousarray(v)
        arrays[name + "_dram"] = v
        aps[name] = nc.dram_tensor(name + "_dram", v.shape, _mybir.dt.from_np(v.dtype), kind="ExternalInput").ap()
    o = nc.dram_tensor("out_dram", (N, F), F32, kind="ExternalOutput").ap()
    build(nc, aps, o, LAYERS)
    r = _run(nc, [arrays], core_ids=[0])
    return r.results[0]["out_dram"]
```

```python
from contextlib import ExitStack

import concourse.bass as bass
from concourse import mybir

F32 = mybir.dt.float32
I32 = mybir.dt.int32
I16 = mybir.dt.int16
BF16 = mybir.dt.bfloat16
ALU = mybir.AluOpType
ACT = mybir.ActivationFunctionType
AX = mybir.AxisListType
RMAX = bass.bass_isa.ReduceOp.max

N = 4096
F = 256
P = 128
NB = N // P
KC = F // P
BANK = 512
EPS = 1e-5
SLOPE = 0.2
POS = 1.0 - SLOPE
CAP = 70.0
IT = 1024
NIT = N // IT
IB = IT // P
UN = 8
NF = 6
R = 16
GN = N // R
IT2 = BANK
NIT2 = N // IT2
G2 = IT2 // R
JP = 256
NH2 = 8
KD = NF * R
KM = KD + R + NH2 + 1
BIG = 1e9
SHIFT = 60.0


def chained(eng, sem):
    count = [0]

    def run(ins):
        count[0] += 1
        ins.then_inc(sem, 1)
        eng.wait_ge(sem, count[0])
    return run


def prepare(nc, sem, ps, keep, layer):
    name, nh, d, src, norm = layer["name"], layer["nh"], layer["d"], layer["src"], layer["norm"]
    C = F + 2 * nh
    proj = layer.get("proj")
    x, mean_v, ident, ones = keep["x"], keep["mean_v"], keep["ident"], keep["ones"]
    s_w, s_vec = sem("weights_in"), sem("vectors_in")
    s_wcat, s_link = sem("weights_ready"), sem("prep_chain")
    s_st, s_var, s_std, s_rstd = sem("row_stats"), sem("variance"), sem("deviation"), sem("rstd")
    s_h, s_t, s_tc, s_p, s_hs = sem("rows"), sem("turned_psum"), sem("turned"), sem("projected"), sem("kept")
    s_pm, s_M, s_dq, s_q, s_aux = sem("part_max"), sem("max_all"), sem("shifted"), sem("q"), sem("aux_ready")
    s_vs, s_vm, s_fi, s_ft, s_fit = sem("value_sums"), sem("mean_psum"), sem("fi"), sem("fi_psum"), sem("fi_rows")
    s_out, s_xa = sem("prep_out"), sem("x_added")
    pair = layer.get("pair")
    s_pc, s_cM, s_rt, s_rrow = sem("curv_part_max"), sem("curv_max"), sem("bound"), sem("bound_rows")
    e = d + 1 if pair else d

    def values(t):
        return t[:, :, 0:nh * e].rearrange("p b (h e) -> p b h e", e=e)[:, :, :, 0:d]

    def icols(t):
        return t[:, :, 0:nh * e].rearrange("p b (h e) -> p b h e", e=e)[:, :, :, d] if pair else t[:, :, F + nh:C]

    def jcols(t):
        return t[:, :, F + nh:C] if pair else t[:, :, F:F + nh]
    FK = max(1, nh * NB // P)
    FR = min(P, nh * NB)
    with ExitStack() as ctx:
        def sb(what, shape):
            return ctx.enter_context(nc.sbuf_tensor(f"{name}_{what}", shape, F32))
        hs = sb("hs", [P, NB, C])
        wcat = sb("wcat", [P, KC, C])
        vecs = sb("vecs", [P, 2, F])
        wtmp = sb("wtmp", [P, KC, F])
        rows = sb("rows", [P, 4, F])
        turned = sb("turned", [P, 2, F])
        st = sb("st", [P, NB, 6])
        sm = sb("sm", [P, 6, NB])
        pm = sb("pm", [P, nh])
        M = sb("M", [P, nh])
        cap = sb("cap", [P, nh])
        vsum = sb("vsum", [P, F])
        q = sb("q", [P, NB, nh])
        fi = sb("fi", [P, NB, nh])
        fit = sb("fit", [P, FK, P])
        if proj:
            wproj = sb("wproj", [P, KC, F])
            pbias = sb("pbias", [P, 2, F])
        if pair:
            curv = sb("curv", [P, NB, NF])
            cmax = sb("cmax", [P, 2, NF])
            gw = sb("gw", [P, nh, NF])
            gate = sb("gate", [P, 1])
            far = sb("far", [P, 2, NB * NF])
            prod = sb("prod", [P, NB, nh * NF])
            bound = sb("bound", [P, 3, NB * nh])
            boundt = sb("boundt", [P, 2 * FK, P])
            wrow = sb("wrow", [P, nh, NF])
        rstd, shift = sm[:, 4, :], sm[:, 5, :]
        block = ctx.enter_context(nc.Block())

        @block.sync
        def _(sp):
            for c in range(KC):
                sp.dma_start(values(wcat)[:, c], layer["w"][c * P:(c + 1) * P, :].rearrange("p (h d) -> p h d", h=nh)
                             ).then_inc(s_w, 16)
            if pair:
                sp.dma_start(pair["x_rows"].rearrange("(b p) f -> p b f", p=P), x[:]).then_inc(s_out, 16)
            if nh > 1:
                sp.dma_start(vecs[:, 0, :], layer["jvec"].partition_broadcast(P)).then_inc(s_vec, 16)
                sp.dma_start(vecs[:, 1, :], layer["ivec"].partition_broadcast(P)).then_inc(s_vec, 16)
            else:
                for c in range(KC):
                    for col, vec in ((F, "jvec"), (F + 1, "ivec")):
                        sp.dma_start(wcat[:, c, col:col + 1],
                                     layer[vec][c * P:(c + 1) * P].unsqueeze(1)).then_inc(s_vec, 16)
            if proj:
                sp.dma_start(wproj[:], proj["w"].rearrange("(c p) n -> p c n", p=P)).then_inc(s_w, 16)
                for k in range(2):
                    sp.dma_start(pbias[:, k, :], proj["bias"][k].partition_broadcast(P)).then_inc(s_vec, 16)
            if pair:
                sp.dma_start(curv[:], pair["curv"].rearrange("(b p) f -> p b f", p=P)).then_inc(s_vec, 16)
                sp.dma_start(gw[:].rearrange("p h f -> p (h f)"),
                             pair["wc"].rearrange("h f -> (h f)").partition_broadcast(P)).then_inc(s_vec, 16)
                sp.dma_start(gate[:], pair["gate"].partition_broadcast(P)).then_inc(s_vec, 16)
            for k in range(4):
                part = slice(k * NB // 4, (k + 1) * NB // 4)
                sp.wait_ge(s_aux, k + 1)
                sp.dma_start(layer["aux"][part].rearrange("b p c -> p b c"), hs[:, part, :]).then_inc(s_out, 16)
            sp.wait_ge(s_fit, FK)
            irow = layer["irow"].rearrange("b h n -> (b h) n")
            for k in range(FK):
                sp.dma_start(irow[k * FR:(k + 1) * FR, :], fit[0:FR, k, :]).then_inc(s_out, 16)
            if pair:
                sp.wait_ge(s_rrow, 2 * FK)
                brow = pair["brow"].rearrange("b h n -> (b h) n")
                krow = pair["krow"].rearrange("b h n -> (b h) n")
                for k in range(FK):
                    sp.dma_start(brow[k * P:(k + 1) * P, :], boundt[:, k, :]).then_inc(s_out, 16)
                    sp.dma_start(krow[k * P:(k + 1) * P, :], boundt[:, FK + k, :]).then_inc(s_out, 16)
                sp.wait_ge(s_out, 16 + 16 * 4 + 48 * FK)
            else:
                sp.wait_ge(s_out, 16 * 4 + 16 * FK)

        @block.gpsimd
        def _(pool):
            pool.wait_ge(s_pm, 1)
            pool.partition_all_reduce(M[:], pm[:], P, RMAX).then_inc(s_M, 1)
            if pair:
                pool.wait_ge(s_pc, 1)
                pool.partition_all_reduce(cmax[:], cmax[:], P, RMAX).then_inc(s_cM, 1)

        @block.scalar
        def _(act):
            if norm:
                act.wait_ge(s_var, 1)
                act.activation(sm[:, 3, :], sm[:, 2, :], ACT.Sqrt).then_inc(s_std, 1)
                act.wait_ge(s_rstd, 1)

            def normalise(b, k):
                act.wait_ge(s_t, b + 1)
                row = src[:, bass.ds(b, 1), :].rearrange("p a c -> p (a c)")
                if norm:
                    act.activation(rows[:, k, :], row, ACT.Relu, bias=shift[:, bass.ds(b, 1)],
                                   scale=rstd[:, bass.ds(b, 1)]).then_inc(s_h, 1)
                else:
                    act.copy(rows[:, k, :], row).then_inc(s_h, 1)

            def turn(t, last):
                for k in range(4):
                    if k < 2 or not last:
                        normalise(t * 4 + k + 2, (k + 2) % 4)
                    act.wait_ge(s_p, t * 4 + k + 3)
                    act.copy(hs[:, bass.ds(t * 4 + k, 1), :].rearrange("p a c -> p (a c)"),
                             ps[:, 2 + k % 2, 0:C]).then_inc(s_hs, 1)

            normalise(0, 0)
            normalise(1, 1)
            with act.Fori(0, NB // 4 - 1) as t:
                turn(t, False)
            turn(NB // 4 - 1, True)
            act.wait_ge(s_dq, 1)
            act.activation(q[:], q[:], ACT.Exp, scale=SLOPE).then_inc(s_q, 1)

        @block.tensor
        def _(pe):
            pe.sem_inc(s_t, 4)
            pe.sem_inc(s_p, 2)
            pe.wait_ge(s_w, 16 * KC + (16 if proj else 0))
            pe.wait_ge(s_wcat, 1)

            def transpose_rows(b, k):
                pe.wait_ge(s_h, b + 1)
                for c in range(KC):
                    ins = pe.transpose(ps[:, k % 2, c * P:(c + 1) * P], rows[:, k, c * P:(c + 1) * P], ident[:])
                ins.then_inc(s_t, 1)

            def turn(t, last):
                for k in range(4):
                    if k < 3 or not last:
                        transpose_rows(t * 4 + k + 1, (k + 1) % 4)
                    pe.wait_ge(s_tc, t * 4 + k + 1)
                    pe.wait_ge(s_hs, t * 4 + k + 1)
                    for c in range(KC):
                        ins = pe.matmul(ps[:, 2 + k % 2, 0:C], turned[:, k % 2, c * P:(c + 1) * P], wcat[:, c, :],
                                        start=c == 0, stop=c == KC - 1)
                    if proj:
                        pe.wait_ge(s_xa, t * 4 + k + 1)
                        for c in range(KC):
                            ins = pe.matmul(ps[:, 4 + k % 2, 0:F], turned[:, k % 2, c * P:(c + 1) * P], wproj[:, c, :],
                                            start=c == 0, stop=c == KC - 1)
                    ins.then_inc(s_p, 1)

            transpose_rows(0, 0)
            with pe.Fori(0, NB // 4 - 1) as t:
                turn(t, False)
            turn(NB // 4 - 1, True)
            pe.wait_ge(s_vs, 1)
            pe.matmul(ps[:, 6, 0:F], ones[:], vsum[:], start=True, stop=True).then_inc(s_vm, 1)
            pe.wait_ge(s_fi, 1)
            flat = fi[:].rearrange("p b h -> p (b h)")
            for k in range(FK):
                pe.transpose(ps[0:FR, 7, k * P:(k + 1) * P], flat[:, k * FR:(k + 1) * FR], ident[:]).then_inc(s_ft, 1)
            if pair:
                pe.wait_ge(s_rt, 1)
                for r in range(2):
                    for k in range(FK):
                        pe.transpose(ps[:, 5, (r * FK + k) * P:(r * FK + k + 1) * P],
                                     bound[:, r, k * P:(k + 1) * P], ident[:]).then_inc(s_ft, 1)

        @block.vector
        def _(dve):
            link = chained(dve, s_link)
            dve.sem_inc(s_hs, 2)
            dve.sem_inc(s_xa, 2)
            if nh > 1:
                dve.wait_ge(s_w, 16 * KC)
                dve.wait_ge(s_vec, 64 if proj else 80 if pair else 32)
                for k in range(2):
                    w4 = wtmp[:].rearrange("p c (h d) -> p c h d", d=d)
                    link(dve.tensor_tensor(w4, values(wcat), vecs[:, k, :].rearrange("p (h d) -> p h d", d=d)
                                           .unsqueeze(1).broadcast_to([P, KC, nh, d]), ALU.mult))
                    link(dve.tensor_reduce((jcols if k == 0 else icols)(wcat), w4, AX.X, ALU.add))
                if proj:
                    link(dve.tensor_tensor(pbias[:, 0, :], pbias[:, 0, :], pbias[:, 1, :], ALU.add))
            else:
                dve.wait_ge(s_vec, 16 * 2 * KC)
            dve.nop().then_inc(s_wcat, 1)
            if norm:
                with dve.Fori(0, NB) as b:
                    dve.bn_stats(st[:, bass.ds(b, 1), :].rearrange("p a c -> p (a c)"),
                                 src[:, bass.ds(b, 1), :].rearrange("p a c -> p (a c)")).then_inc(s_st, 1)
                dve.wait_ge(s_st, NB)
                link(dve.tensor_tensor(sm[:, 0, :], st[:, :, 1], st[:, :, 4], ALU.add))
                link(dve.tensor_tensor(sm[:, 1, :], st[:, :, 1], st[:, :, 4], ALU.subtract))
                link(dve.tensor_tensor(sm[:, 1, :], sm[:, 1, :], sm[:, 1, :], ALU.mult))
                link(dve.tensor_tensor(sm[:, 2, :], st[:, :, 2], st[:, :, 5], ALU.add))
                link(dve.scalar_tensor_tensor(sm[:, 2, :], sm[:, 1, :], F / 4.0, sm[:, 2, :], ALU.mult, ALU.add))
                dve.tensor_scalar(sm[:, 2, :], sm[:, 2, :], 1.0 / F, EPS, ALU.mult, ALU.add).then_inc(s_var, 1)
                dve.wait_ge(s_std, 1)
                link(dve.reciprocal(rstd, sm[:, 3, :]))
                dve.scalar_tensor_tensor(shift, sm[:, 0, :], -0.5, rstd, ALU.mult, ALU.mult).then_inc(s_rstd, 1)

            def copy_turned(b, k):
                dve.wait_ge(s_t, b + 5)
                dve.wait_ge(s_p, b + 1)
                dve.tensor_copy(turned[:, k % 2, :], ps[:, k % 2, 0:F]).then_inc(s_tc, 1)

            def turn(t, last):
                for k in range(4):
                    if k < 3 or not last:
                        copy_turned(t * 4 + k + 1, k + 1)
                    if proj:
                        dve.wait_ge(s_p, t * 4 + k + 3)
                        xb = x[:, bass.ds(t * 4 + k, 1), :].rearrange("p a c -> p (a c)")
                        dve.tensor_tensor(xb, xb, ps[:, 4 + k % 2, 0:F], ALU.add).then_inc(s_xa, 1)

            copy_turned(0, 0)
            with dve.Fori(0, NB // 4 - 1) as t:
                turn(t, False)
            turn(NB // 4 - 1, True)
            dve.wait_ge(s_hs, NB + 2)
            if proj:
                dve.wait_ge(s_xa, NB + 2)
                link(dve.tensor_tensor(x[:], x[:], pbias[:, 0, :].unsqueeze(1).broadcast_to([P, NB, F]), ALU.add))
            dve.tensor_reduce(pm[:], jcols(hs).rearrange("p b c -> p c b"), AX.X, ALU.max).then_inc(s_pm, 1)
            dve.tensor_reduce(vsum[:].rearrange("p (h d) -> p h d", d=d), values(hs).rearrange("p b h d -> p h d b"),
                              AX.X, ALU.add).then_inc(s_vs, 1)
            dve.wait_ge(s_M, 1)
            dve.tensor_tensor(q[:], jcols(hs), M[:].unsqueeze(1).broadcast_to([P, NB, nh]),
                              ALU.subtract).then_inc(s_dq, 1)
            if pair:
                link(dve.memset(cap[:], 3e38))
            else:
                link(dve.tensor_scalar(cap[:], M[:], -POS, CAP, ALU.mult, ALU.add))
            dve.scalar_tensor_tensor(fi[:], icols(hs), POS, cap[:].unsqueeze(1).broadcast_to([P, NB, nh]),
                                     ALU.mult, ALU.min).then_inc(s_fi, 1)
            dve.wait_ge(s_vm, 1)
            link(dve.tensor_copy(mean_v[:], ps[:, 6, 0:F]))
            if pair:
                link(dve.tensor_scalar(far[:, 0, :], curv[:].rearrange("p b f -> p (b f)"), -1.0, None, ALU.mult))
                link(dve.tensor_reduce(cmax[:, 0, :], curv[:].rearrange("p b f -> p f b"), AX.X, ALU.max))
                dve.tensor_reduce(cmax[:, 1, :], far[:, 0, :].rearrange("p (b f) -> p f b", f=NF),
                                  AX.X, ALU.max).then_inc(s_pc, 1)
                link(dve.tensor_scalar(wrow[:], gw[:], gate[:, 0:1], None, ALU.mult))
                link(dve.tensor_scalar(gw[:], wrow[:], 0.0, None, ALU.max))
                dve.wait_ge(s_cM, 1)
                f0 = far[:, 0, :].rearrange("p (b f) -> p b f", f=NF)
                f1 = far[:, 1, :].rearrange("p (b f) -> p b f", f=NF)
                link(dve.tensor_tensor(f0, f0, cmax[:, 0:1, :].broadcast_to([P, NB, NF]), ALU.add))
                link(dve.tensor_tensor(f1, curv[:], cmax[:, 1:2, :].broadcast_to([P, NB, NF]), ALU.add))
                link(dve.tensor_tensor(f0, f0, f1, ALU.max))
                pr = prod[:].rearrange("p b (h f) -> p b h f", f=NF)
                link(dve.tensor_tensor(pr, f0.unsqueeze(2).broadcast_to([P, NB, nh, NF]),
                                       gw[:].unsqueeze(1).broadcast_to([P, NB, nh, NF]), ALU.mult))
                b3 = [bound[:, k, :].rearrange("p (b h) -> p b h", h=nh) for k in range(3)]
                link(dve.tensor_reduce(b3[1], pr, AX.X, ALU.add))
                link(dve.tensor_tensor(b3[2], icols(hs), M[:].unsqueeze(1).broadcast_to([P, NB, nh]), ALU.add))
                link(dve.tensor_scalar(bound[:, 2, :], bound[:, 2, :], 0.0, -POS, ALU.max, ALU.mult))
                link(dve.tensor_tensor(bound[:, 0, :], bound[:, 2, :], bound[:, 1, :], ALU.subtract))
                link(dve.tensor_tensor(pr, curv[:].unsqueeze(2).broadcast_to([P, NB, nh, NF]),
                                       wrow[:].unsqueeze(1).broadcast_to([P, NB, nh, NF]), ALU.mult))
                link(dve.tensor_reduce(b3[2], pr, AX.X, ALU.add))
                link(dve.tensor_scalar(bound[:, 1, :], bound[:, 2, :], -1.0, None, ALU.mult))
                link(dve.scalar_tensor_tensor(bound[:, 0, :], bound[:, 0, :], SHIFT, bound[:, 2, :], ALU.add, ALU.add))
                dve.nop().then_inc(s_rt, 1)
            dve.wait_ge(s_q, 1)
            link(dve.tensor_scalar(jcols(hs), jcols(hs), POS, None, ALU.mult))
            link(dve.tensor_copy(icols(hs), q[:]))
            for k in range(4):
                part = slice(k * NB // 4, (k + 1) * NB // 4)
                v = values(hs)[:, part]
                dve.tensor_tensor(v, v, q[:, part, :].unsqueeze(3).broadcast_to([P, NB // 4, nh, d]),
                                  ALU.mult).then_inc(s_aux, 1)
            dve.wait_ge(s_ft, FK)
            for k in range(FK):
                dve.tensor_copy(fit[0:FR, k, :], ps[0:FR, 7, k * P:(k + 1) * P]).then_inc(s_fit, 1)
            if pair:
                dve.wait_ge(s_ft, 3 * FK)
                for k in range(2 * FK):
                    dve.tensor_copy(boundt[:, k, :], ps[:, 5, k * P:(k + 1) * P]).then_inc(s_rrow, 1)


def finish_rows(dve, ps, keep, layer, it, blocks, bank_sums, bank_outs, bufs, sems):
    nh, elu, dst = layer["nh"], layer["elu"], layer.get("dst")
    den, att, tmp = bufs
    s_link, s_ot, s_post, s_mn, s_e = sems
    TB = blocks // 2
    d = F // nh
    links = 4 + TB * (1 + 2 * bool(layer["mean"]) + elu * (2 if dst is None else 1))
    count = [0]

    def link(ins):
        count[0] += 1
        ins.then_inc(s_link, 1)
        dve.wait_ge(s_link, it * links + count[0])
    sums = ps[:, bank_sums:bank_sums + 2, :].rearrange("p a (m r) -> p (a m) r", r=32)[:, :, 0]
    if nh > 1:
        link(dve.tensor_copy(den[:, 0].rearrange("p b h -> p (b h)"), sums))
    else:
        link(dve.tensor_reduce(den[:, 0].rearrange("p b h -> p (b h)"), sums.rearrange("p (b g) -> p b g", g=4),
                               AX.X, ALU.add))
    link(dve.tensor_scalar(den[:, 1], den[:, 0], 0.0, None, ALU.is_equal))
    link(dve.tensor_tensor(den[:, 2], den[:, 0], den[:, 1], ALU.add))
    link(dve.reciprocal(den[:, 3], den[:, 2]))
    wide = [P, 2, nh, d]
    a4 = att[:].rearrange("p b (h d) -> p b h d", h=nh)
    t4 = tmp[:].rearrange("p b (h d) -> p b h d", h=nh)
    m4 = keep["mean_v"][:].rearrange("p (h d) -> p h d", h=nh).unsqueeze(1).broadcast_to(wide)
    for r in range(TB):
        dve.wait_ge(s_ot, it * TB + r + 1)
        o = ps[:, bank_outs + r % 2, :].rearrange("p (b h d) -> p b h d", b=2, h=nh)
        rec = den[:, 3, 2 * r:2 * r + 2, :].unsqueeze(3).broadcast_to(wide)
        dve.tensor_tensor(a4, o, rec, ALU.mult).then_inc(s_post, 1)
        if layer["mean"]:
            none = den[:, 1, 2 * r:2 * r + 2, :].unsqueeze(3).broadcast_to(wide)
            link(dve.tensor_tensor(t4, m4, none, ALU.mult))
        dve.wait_ge(s_post, it * TB + r + 3)
        if layer["mean"]:
            link(dve.tensor_tensor(att[:], att[:], tmp[:], ALU.add))
        rows = (dst if dst is not None else keep["x"])[:, bass.ds(it * blocks + 2 * r, 2), :]
        if elu:
            dve.tensor_scalar(tmp[:], att[:], 0.0, None, ALU.min).then_inc(s_mn, 1)
            link(dve.tensor_scalar(att[:], att[:], 0.0, -1.0, ALU.max, ALU.add))
            dve.wait_ge(s_e, it * TB + r + 1)
            if dst is None:
                link(dve.tensor_tensor(att[:], att[:], tmp[:], ALU.add))
                link(dve.tensor_tensor(rows, rows, att[:], ALU.add))
            else:
                link(dve.tensor_tensor(rows, att[:], tmp[:], ALU.add))
        else:
            link(dve.tensor_tensor(rows, rows, att[:], ALU.add))
    assert count[0] == links, (count[0], links)


def attend(nc, sem, ps, keep, layer, adj_t):
    name, nh, elu, dst = layer["name"], layer["nh"], layer["elu"], layer.get("dst")
    x, mean_v, ident, zeros = keep["x"], keep["mean_v"], keep["ident"], keep["zeros"]
    C = F + 2 * nh
    G = 1 if nh > 1 else 4
    RING = 4 if nh > 1 else 8
    CR = RING // G
    DEN = 4
    TB = IB // 2
    s_in = [sem(f"tile_in{k}") for k in range(RING)]
    s_fi, s_u, s_p, s_pv = sem("fi_in"), sem("exps"), sem("weights"), sem("contracted")
    s_acc, s_ev, s_dt, s_ot, s_post = sem("tile_done"), sem("evacuated"), sem("sums_turned"), sem("outs_turned"), sem("outs_used")
    s_link, s_mn, s_e = sem("post_chain"), sem("negatives"), sem("elu_exp")
    mask, nonzero = layer.get("mask"), layer.get("nonzero")
    s_sign, s_a16, s_ed = sem("signs"), sem("adj_16_bits"), sem("edges")
    s_ri, s_rc, s_ro = sem("adj_rows_in"), sem("adj_rows_less_1"), sem("adj_rows_out")
    s_rf = sem("adj_rows_free")
    with ExitStack() as ctx:
        def sb(what, shape, dt=F32):
            return ctx.enter_context(nc.sbuf_tensor(f"{name}_att_{what}", shape, dt))
        fi = sb("fi", [P, nh, IT])
        adj = sb("adj", [P, RING, IT], I32)
        aux = sb("aux", [P, RING, C])
        u = sb("u", [P, 4, IT])
        w = sb("w", [P, 8, IT])
        ot = sb("ot", [P, 6, BANK])
        den = sb("den", [P, 4, IB, nh])
        att = sb("att", [P, 2, F])
        tmp = sb("tmp", [P, 2, F])
        if nonzero:
            edges = sb("edges", [P, nh, IT], I16)
            adj16 = sb("adj16", [P, 2, IT], I16)
        if mask:
            arows = sb("arows", [P, N], I32)
        block = ctx.enter_context(nc.Block())

        @block.sync
        def _(sp):
            with sp.Fori(0, NIT) as it:
                if nonzero:
                    sp.wait_ge(s_sign, it * (nh * NB) + 1)
                else:
                    sp.wait_ge(s_u, it * (nh * NB) + 1)
                for h in range(nh):
                    sp.dma_start(fi[:, h, :].rearrange("p (b n) -> p b n", n=P),
                                 layer["irow"][bass.ds(it * IB, IB), h, :].partition_broadcast(P)).then_inc(s_fi, 16)
                with sp.Fori(0, NB // UN) as t:
                    for k in range(UN):
                        j = t * UN + k
                        g = it * (NB // G) + t * (UN // G) + k // G
                        if mask and k == 3:
                            row = it * (NB // UN) + t
                            sp.wait_ge(s_rf, row + 1)
                            sp.dma_start(arows[:], mask["adj"][bass.ds(row * P + mask["first"] * P, P), :]
                                         ).then_inc(s_ri, 16)
                        sp.wait_ge(s_pv, g + 1)
                        sp.dma_start(adj[:, k % RING, :],
                                     adj_t[bass.ds(j * P, P), bass.ds(it * IT, IT)]).then_inc(s_in[k % RING], 16)
                        sp.dma_start(aux[:, k % RING, :],
                                     layer["aux"][bass.ds(j, 1), :, :].rearrange("a p c -> (a p) c")
                                     ).then_inc(s_in[k % RING], 16)

        @block.scalar
        def _(act):
            act.sem_inc(s_u, 1)
            if nonzero:
                act.sem_inc(s_sign, 1)
            with act.Fori(0, NIT) as it:
                act.wait_ge(s_fi, it * (16 * nh) + 16 * nh)
                with act.Fori(0, NB // UN) as t:
                    for k in range(UN):
                        act.wait_ge(s_in[k % RING], (it * (NB // RING) + t * (UN // RING) + k // RING + 1) * 32)
                        for h in range(nh):
                            n = (it * NB + t * UN + k) * nh + h
                            act.wait_ge(s_p, n + 1)
                            act.activation(u[:, (k * nh + h) % 4, :], fi[:, h, :], ACT.Exp,
                                           bias=aux[:, k % RING, F + h:F + h + 1]).then_inc(s_u, 1)
                            if nonzero:
                                act.activation(edges[:, h, :], fi[:, h, :], ACT.Sign,
                                               bias=aux[:, k % RING, F + h:F + h + 1]).then_inc(s_sign, 1)
                act.wait_ge(s_acc, it + 1)
                for c in range(3):
                    act.copy(ot[:, c, :], ps[:, c, :]).then_inc(s_ev, 1)
                if elu:
                    for r in range(TB):
                        act.wait_ge(s_mn, it * TB + r + 1)
                        act.activation(tmp[:], tmp[:], ACT.Exp).then_inc(s_e, 1)

        @block.gpsimd
        def _(pool):
            if mask:
                pool.sem_inc(s_rf, 1)
                with pool.Fori(0, NIT * NB // UN) as row:
                    pool.wait_ge(s_rc, row * 4 + 4)
                    pool.dma_start(mask["less_1"][bass.ds(row * P + mask["first"] * P, P), :],
                                   arows[:].bitcast(F32)).then_inc(s_ro, 16)
                    pool.wait_ge(s_ro, row * 16 + 16)
                    pool.sem_inc(s_rf, 1)

        @block.vector
        def _(dve):
            dve.sem_inc(s_p, 4)
            dve.sem_inc(s_post, 2)
            with dve.Fori(0, NIT) as it:
                with dve.Fori(0, NB // UN) as t:
                    for k in range(UN):
                        g = it * (NB // G) + t * (UN // G) + k // G
                        if mask and 2 <= k < 6:
                            if k == 2:
                                dve.wait_ge(s_ri, (it * (NB // UN) + t) * 16 + 16)
                            piece = arows[:, (k - 2) * IT:(k - 1) * IT]
                            dve.tensor_scalar(piece.bitcast(F32), piece, -1.0, None, ALU.add).then_inc(s_rc, 1)
                        if nonzero:
                            j = it * NB + t * UN + k
                            dve.wait_ge(s_u, j * nh + 2)
                            dve.tensor_copy(adj16[:, k % 2, :], adj[:, k % RING, :]).then_inc(s_a16, 1)
                            dve.wait_ge(s_a16, j + 1)
                        dve.wait_ge(s_pv, g + 1 + CR - 2)
                        for h in range(nh):
                            n = (it * NB + t * UN + k) * nh + h
                            dve.wait_ge(s_u, n + 2)
                            edge = adj[:, k % RING, :]
                            if nonzero:
                                edge = edges[:, h, :]
                                if h % 2 == 0:
                                    dve.wait_ge(s_sign, n + 3)
                                    two = edges[:, h:h + 2, :]
                                    dve.tensor_tensor(two, two, adj16[:, k % 2:k % 2 + 1, :].broadcast_to([P, 2, IT]),
                                                      ALU.bitwise_and).then_inc(s_ed, 1)
                                    dve.wait_ge(s_ed, (it * NB + t * UN + k) * (nh // 2) + h // 2 + 1)
                            dve.scalar_tensor_tensor(w[:, (k * nh + h) % 8, :], u[:, (k * nh + h) % 4, :], 1.0,
                                                     edge, ALU.max, ALU.mult).then_inc(s_p, 1)
                dve.wait_ge(s_acc, it + 1)
                for c in range(3, 6):
                    dve.tensor_copy(ot[:, c, :], ps[:, c, :]).then_inc(s_ev, 1)
                dve.wait_ge(s_dt, it + 1)
                finish_rows(dve, ps, keep, layer, it, IB, 6, 4, (den, att, tmp), (s_link, s_ot, s_post, s_mn, s_e))

        @block.tensor
        def _(pe):
            pe.sem_inc(s_pv, CR)
            with pe.Fori(0, NIT) as it:
                pe.wait_ge(s_post, it * TB + 2)
                for c in range(6):
                    pe.matmul(ps[:, c, :], zeros[:, 0:P], zeros[:], start=True, stop=False, skip_group_check=True)
                with pe.Fori(0, NB // UN) as t:
                    for k in range(UN):
                        n = (it * NB + t * UN + k) * nh
                        a = aux[:, k % RING, :]
                        if nh > 1:
                            for pair in range(nh // 2):
                                pe.wait_ge(s_p, n + 2 * pair + 6)
                                for c in range(2):
                                    for e in range(2):
                                        h = 2 * pair + e
                                        pe.matmul(ps[64 * e:64 * e + 64, 2 * pair + c, :], a[:, 64 * h:64 * h + 64],
                                                  w[:, (k * nh + h) % 8, c * BANK:(c + 1) * BANK],
                                                  start=False, stop=False, skip_group_check=True)
                        else:
                            pe.wait_ge(s_p, n + 5)
                            for half in range(2):
                                for c in range(2):
                                    pe.matmul(ps[:, 2 * half + c, :], a[:, half * P:(half + 1) * P],
                                              w[:, k, c * BANK:(c + 1) * BANK],
                                              start=False, stop=False, skip_group_check=True)
                        if (k + 1) % G == 0:
                            for c in range(2):
                                for e in range(4):
                                    kk, h = (k, e) if nh > 1 else (k - 3 + e, 0)
                                    q = aux[:, kk % RING, F + nh + h:F + nh + h + 1].broadcast_to([P, 32])
                                    ins = pe.matmul(ps[32 * e:32 * e + 32, DEN + c, :], q,
                                                    w[:, (kk * nh + h) % 8, c * BANK:(c + 1) * BANK],
                                                    start=False, stop=False, skip_group_check=True)
                            ins.then_inc(s_pv, 1)
                for c in range(6):
                    ins = pe.matmul(ps[:, c, :], zeros[:, 0:P], zeros[:], start=False, stop=True, skip_group_check=True)
                ins.then_inc(s_acc, 1)
                pe.wait_ge(s_ev, it * 6 + 6)
                for b in range(IB):
                    ins = pe.transpose(ps[:, 6 + b // 4, (b % 4) * P:(b % 4 + 1) * P],
                                       ot[:, DEN + b // 4, (b % 4) * P:(b % 4 + 1) * P], ident[:])
                ins.then_inc(s_dt, 1)
                for r in range(TB):
                    pe.wait_ge(s_post, it * TB + r + 1)
                    for e in range(2):
                        b = 2 * r + e
                        for half in range(2):
                            ins = pe.transpose(ps[:, 4 + r % 2, e * F + half * P:e * F + (half + 1) * P],
                                               ot[:, 2 * half + b // 4, (b % 4) * P:(b % 4 + 1) * P], ident[:])
                    ins.then_inc(s_ot, 1)


def attend_pairwise(nc, sem, ps, keep, layer):
    name, nh, pair = layer["name"], layer["nh"], layer["pair"]
    x, mean_v, ident, zeros = keep["x"], keep["mean_v"], keep["ident"], keep["zeros"]
    C = F + 2 * nh
    d = F // nh
    TJ = 4
    NT = NB // TJ
    CG = 2 * BANK // P
    NCH = G2 // CG
    IB2 = IT2 // P
    PARTS = 2 * NCH
    PG = G2 // PARTS
    OUT = 4
    s_in = [sem(f"aux_in{k}") for k in range(TJ)]
    s_m = [sem(f"edges_in{k}") for k in range(2)]
    s_c, s_c2, s_cc, s_fi, s_r, s_d, s_l = (sem("constants_in"), sem("coefficients"), sem("ones_set"), sem("fi_in"),
                                            sem("shift_in"), sem("differences"), sem("relus"))
    s_b, s_t, s_e, s_pv = sem("bias_psum"), sem("logits"), sem("weights"), sem("contracted")
    s_acc, s_ev, s_ot, s_post, s_link = (sem("tile_done"), sem("evacuated"), sem("outs_turned"), sem("outs_used"),
                                         sem("post_chain"))
    s_copy, s_xi, s_xd, s_xo = sem("coefficient_chain"), sem("x_rows_in"), sem("x_rows_done"), sem("x_rows_out")
    with ExitStack() as ctx:
        def sb(what, shape, dt=F32):
            return ctx.enter_context(nc.sbuf_tensor(f"{name}_att_{what}", shape, dt))
        diff = sb("diff", [P, 2, G2, JP])
        coef = sb("coef", [KM, G2, P])
        cj = sb("cj", [KD, N])
        ci = sb("ci", [KD, GN + G2])
        gwr = sb("gwr", [KD, nh])
        gate = sb("gate", [KD, 1])
        fi = sb("fi", [P, nh, IT2])
        w_own = sb("w", [P, 2, nh, IT2])
        aux = sb("aux", [P, TJ, C])
        ot = sb("ot", [P, 4, BANK])
        den = sb("den", [P, 4, IB2, nh])
        att = sb("att", [P, IB2, F])
        tmp = sb("tmp", [P, IB2, F])
        xr = sb("xr", [P, IB2, F])
        xw = x[:].rearrange("p (k b) f -> p k (b f)", k=2).rearrange("p k (h n) -> p k h n", h=nh)
        w = [xw[:, 0], xw[:, 1], w_own[:, 0], w_own[:, 1]]
        x_rows = pair["x_rows"].rearrange("(b p) f -> p b f", p=P)
        block = ctx.enter_context(nc.Block())

        @block.sync
        def _(sp):
            for f in range(NF):
                part = slice(f * R, (f + 1) * R)
                sp.dma_start(cj[part, :], pair["curv_t"][f, :].partition_broadcast(R)).then_inc(s_c, 16)
                sp.dma_start(gwr[part, :], pair["wc_t"][f, :].partition_broadcast(R)).then_inc(s_c, 16)
            sp.dma_start(ci[:, 0:GN], pair["curv_g"]).then_inc(s_c, 16)
            sp.dma_start(gate[:], pair["gate"].partition_broadcast(KD)).then_inc(s_c, 16)
            sp.dma_start(coef[0:KD, 0, :], pair["same_i"][0:KD, :]).then_inc(s_c, 16)
            sp.dma_start(coef[KD:KM - 1, :, :], pair["same_i"][KD:KM - 1, :].unsqueeze(1)
                         .broadcast_to([R + nh, G2, P])).then_inc(s_c, 16)
            sp.wait_ge(s_cc, 1)
            with sp.Fori(0, NIT2) as it:
                sp.wait_ge(s_xd, it + 1)
                sp.dma_start(xr[:], x_rows[:, bass.ds(it * IB2, IB2), :]).then_inc(s_xi, 16)
                sp.wait_ge(s_l, it * NB + 1)
                for h in range(nh):
                    sp.dma_start(fi[:, h, :].rearrange("p (b n) -> p b n", n=P),
                                 layer["irow"][bass.ds(it * IB2, IB2), h, :].partition_broadcast(P)).then_inc(s_fi, 16)
                sp.wait_ge(s_b, it * (NB * NCH) + 16)
                for b in range(IB2):
                    sp.dma_start(coef[KM - 1:KM, b * 8:(b + 1) * 8, :].rearrange("p g (h n) -> p g h n", n=R),
                                 pair["brow"][bass.ds(it * IB2 + b, 1), :, :].rearrange("a h (g n) -> a g h n", n=R)
                                 ).then_inc(s_r, 16)
                with sp.Fori(0, NT) as t:
                    for k in range(TJ):
                        n = it * NB + t * TJ + k
                        e = k // 2
                        if k % 2 == 0:
                            dp = it * (NB // 2) + t * (TJ // 2) + e
                            sp.wait_ge(s_b, dp * (2 * NCH) + 2 * NCH)
                            sp.dma_start(diff[KD:KD + R, e, :, :],
                                         pair["less_1"][bass.ds(it * IT2, IT2), bass.ds(t * (2 * JP) + e * JP, JP)]
                                         .rearrange("(g i) j -> i g j", i=R)).then_inc(s_m[e], 16)
                        sp.dma_start(diff[KD + R:KM - 1, e, :, (k % 2) * P:(k % 2 + 1) * P],
                                     pair["krow"][bass.ds(t * TJ + k, 1), :, :].rearrange("a h n -> (a h) n")
                                     .unsqueeze(1).broadcast_to([nh, G2, P])).then_inc(s_m[e], 16)
                        sp.wait_ge(s_pv, n + 1)
                        sp.dma_start(aux[:, k, :], layer["aux"][bass.ds(t * TJ + k, 1), :, :]
                                     .rearrange("a p c -> (a p) c")).then_inc(s_in[k], 16)
            sp.wait_ge(s_xo, 16 * NIT2)
            sp.dma_start(x[:], x_rows).then_inc(s_xi, 16)
            sp.wait_ge(s_xi, 16 * NIT2 + 16)

        @block.gpsimd
        def _(pool):
            pool.sem_inc(s_xd, 1)
            with pool.Fori(0, NIT2) as it:
                pool.wait_ge(s_ev, it * 5 + 5)
                pool.dma_start(x_rows[:, bass.ds(it * IB2, IB2), :], xr[:]).then_inc(s_xo, 16)
                pool.wait_ge(s_xo, it * 16 + 16)
                pool.sem_inc(s_xd, 1)

        @block.scalar
        def _(act):
            act.sem_inc(s_l, 1)

            def relus(it, t, k):
                n = it * NB + t * TJ + k
                act.wait_ge(s_in[k], (it * NT + t) * 16 + 16)
                for h in range(nh):
                    ins = act.activation(w[k][:, h, :], fi[:, h, :], ACT.Relu, bias=aux[:, k, F + nh + h:F + nh + h + 1])
                ins.then_inc(s_l, 1)

            def turn(it, t, last):
                for k in range(TJ):
                    if k < 2:
                        relus(it, t, k + 2)
                    elif not last:
                        relus(it, t + 1, k - 2)
                    if k == TJ - 1 and last:
                        continue
                    t2, k2 = (t, k + 1) if k + 1 < TJ else (t + 1, 0)
                    exp(it, t2, k2)

            def exp(it, t, k):
                n = it * NB + t * TJ + k
                act.wait_ge(s_t, n * NCH + NCH + 2)
                flat = w[k].rearrange("p h n -> p (h n)")
                act.activation(flat, flat, ACT.Exp).then_inc(s_e, 1)

            with act.Fori(0, NIT2) as it:
                act.wait_ge(s_fi, it * (16 * nh) + 16 * nh)
                relus(it, 0, 0)
                relus(it, 0, 1)
                exp(it, 0, 0)
                with act.Fori(0, NT - 1) as t:
                    turn(it, t, False)
                turn(it, NT - 1, True)
                act.wait_ge(s_acc, it + 1)
                for c in range(2):
                    act.copy(ot[:, c, :], ps[:, OUT + c, :]).then_inc(s_ev, 1)

        @block.vector
        def _(dve):
            dve.sem_inc(s_t, 2)
            dve.sem_inc(s_post, 1)
            dve.memset(ci[:, GN:GN + G2], 0.0).then_inc(s_copy, 1)
            for e in range(2):
                dve.memset(diff[KD:P, e], 1.0).then_inc(s_copy, 1)
            dve.wait_ge(s_copy, 3)
            dve.nop().then_inc(s_cc, 1)
            dve.wait_ge(s_c, 16 * (2 * NF + 4))
            dve.tensor_scalar(gwr[:], gwr[:], gate[:, 0:1], 2.0, ALU.mult, ALU.mult).then_inc(s_copy, 1)
            dve.wait_ge(s_copy, 4)
            c0 = coef[0:KD, 0, :].rearrange("p (h n) -> p h n", n=R)
            dve.tensor_tensor(c0, c0, gwr[:].unsqueeze(2).broadcast_to([KD, nh, R]), ALU.mult).then_inc(s_copy, 1)
            dve.wait_ge(s_copy, 5)
            dve.tensor_copy(coef[0:KD, 1:G2, :], coef[0:KD, 0:1, :].broadcast_to([KD, G2 - 1, P])).then_inc(s_c2, 1)

            def differences(it, t, e, part):
                dp = it * (NB // 2) + t * (TJ // 2) + e
                if part == 0:
                    dve.wait_ge(s_b, dp * (2 * NCH) + 2 * NCH)
                for g in range(part * PG, (part + 1) * PG):
                    ins = dve.tensor_scalar(diff[0:KD, e, g, :], cj[:, bass.ds(t * (2 * JP) + e * JP, JP)],
                                            ci[:, bass.ds(it * G2 + g, 1)], 0.0, ALU.subtract, ALU.max)
                ins.then_inc(s_d, 1)

            def turn(it, t, last):
                for k in range(TJ):
                    n = it * NB + t * TJ + k
                    dve.wait_ge(s_l, n + 2)
                    for c in range(NCH):
                        dve.wait_ge(s_b, n * NCH + c + 1 + 16)
                        l = w[k][:, :, c * P:(c + 1) * P].rearrange("p h (g i) -> p g h i", i=R)
                        bank = 2 * (c % 2)
                        b = ps[:, bank:bank + 2, :].rearrange("p a (g h i) -> p (a g) h i", h=nh, i=R)
                        dve.tensor_tensor(l, b, l, ALU.add).then_inc(s_t, 1)
                        part = (k % 2) * NCH + c
                        if k < 2:
                            differences(it, t, 1, part)
                        elif not last:
                            differences(it, t + 1, 0, part)
                        else:
                            differences(it + 1, 0, 0, part)

            for part in range(PARTS):
                differences(0, 0, 0, part)
            links = 7
            with dve.Fori(0, NIT2) as it:
                with dve.Fori(0, NT - 1) as t:
                    turn(it, t, False)
                turn(it, NT - 1, True)
                dve.wait_ge(s_acc, it + 1)
                for c in range(2, 4):
                    dve.tensor_copy(ot[:, c, :], ps[:, OUT + c, :]).then_inc(s_ev, 1)
                count = [0]

                def link(ins):
                    count[0] += 1
                    ins.then_inc(s_link, 1)
                    dve.wait_ge(s_link, it * links + count[0])
                turned = ps[:, OUT:OUT + IB2, :].rearrange("p b (h m) -> p b h m", m=64)
                wide = [P, IB2, nh, d]
                a4 = att[:].rearrange("p b (h d) -> p b h d", h=nh)
                t4 = tmp[:].rearrange("p b (h d) -> p b h d", h=nh)
                m4 = mean_v[:].rearrange("p (h d) -> p h d", h=nh).unsqueeze(1).broadcast_to(wide)
                dve.wait_ge(s_ot, it + 1)
                link(dve.tensor_copy(den[:, 0], turned[:, :, :, d]))
                link(dve.tensor_scalar(den[:, 1], den[:, 0], 0.0, None, ALU.is_equal))
                link(dve.tensor_tensor(den[:, 2], den[:, 0], den[:, 1], ALU.add))
                link(dve.reciprocal(den[:, 3], den[:, 2]))
                dve.tensor_tensor(a4, turned[:, :, :, 0:d], den[:, 3].unsqueeze(3).broadcast_to(wide),
                                  ALU.mult).then_inc(s_post, 1)
                link(dve.tensor_tensor(t4, m4, den[:, 1].unsqueeze(3).broadcast_to(wide), ALU.mult))
                dve.wait_ge(s_post, it + 2)
                link(dve.tensor_tensor(att[:], att[:], tmp[:], ALU.add))
                dve.wait_ge(s_xi, it * 16 + 16)
                link(dve.tensor_tensor(xr[:], xr[:], att[:], ALU.add))
                dve.nop().then_inc(s_ev, 1)

        @block.tensor
        def _(pe):
            pe.sem_inc(s_b, 16)
            pe.sem_inc(s_pv, TJ)
            pe.wait_ge(s_c2, 1)

            def contract(k, pairs):
                for p in pairs:
                    for e in range(2):
                        h = 2 * p + e
                        ins = pe.matmul(ps[64 * e:64 * e + d + 1, OUT + p, :], aux[:, k, (d + 1) * h:(d + 1) * (h + 1)],
                                        w[k][:, h, :], start=False, stop=False, skip_group_check=True)
                return ins

            def bias_chunk(it, t, k, c):
                n = it * NB + t * TJ + k
                e = k // 2
                if k % 2 == 0 and c == 0:
                    dp = it * (NB // 2) + t * (TJ // 2) + e
                    pe.wait_ge(s_d, dp * PARTS + PARTS)
                if c == 0:
                    pe.wait_ge(s_m[e], (it * NT + t) * 48 + 48)
                pe.wait_ge(s_t, n * NCH + c + 1)
                for g in range(CG):
                    col = (g % 4) * P
                    ins = pe.matmul(ps[:, 2 * (c % 2) + g // 4, col:col + P],
                                    diff[0:KM, e, c * CG + g, (k % 2) * P:(k % 2 + 1) * P],
                                    coef[:, c * CG + g, :], start=True, stop=True)
                ins.then_inc(s_b, 1)

            def turn(it, t, last):
                for k in range(TJ):
                    n = it * NB + t * TJ + k
                    for c in range(NCH):
                        if k < 2:
                            bias_chunk(it, t, k + 2, c)
                        elif not last:
                            bias_chunk(it, t + 1, k - 2, c)
                        if c == 0:
                            pe.wait_ge(s_e, n + 1)
                        ins = contract(k, [c])
                    ins.then_inc(s_pv, 1)

            with pe.Fori(0, NIT2) as it:
                pe.wait_ge(s_r, it * (16 * IB2) + 16 * IB2)
                for k in range(2):
                    for c in range(NCH):
                        bias_chunk(it, 0, k, c)
                pe.wait_ge(s_post, it + 1)
                for c in range(4):
                    pe.matmul(ps[:, OUT + c, :], zeros[:, 0:P], zeros[:], start=True, stop=False, skip_group_check=True)
                with pe.Fori(0, NT - 1) as t:
                    turn(it, t, False)
                turn(it, NT - 1, True)
                for c in range(4):
                    ins = pe.matmul(ps[:, OUT + c, :], zeros[:, 0:P], zeros[:], start=False, stop=True, skip_group_check=True)
                ins.then_inc(s_acc, 1)
                pe.wait_ge(s_ev, it * 5 + 4)
                for b in range(IB2):
                    for p in range(4):
                        ins = pe.transpose(ps[:, OUT + b, p * P:(p + 1) * P], ot[:, p, b * P:(b + 1) * P], ident[:])
                ins.then_inc(s_ot, 1)


def build(nc, a, out, layers):
    with ExitStack() as ctx:
        def sb(name, shape, dt=F32):
            return ctx.enter_context(nc.sbuf_tensor(name, shape, dt))

        def dram(name, shape, dt=F32):
            return nc.dram_tensor(name, shape, dt, kind="Internal").ap()

        def phase(f, prefix, *args):
            made = []

            def sem(name):
                made.append(nc.alloc_semaphore(name=f"{prefix}_{name}"))
                return made[-1]
            f(nc, sem, ps, keep, *args)
            nc.clear_and_free_semaphores(made)
            nc.all_engine_barrier()
        ps = ctx.enter_context(nc.psum_tensor("ps", [P, 8, BANK], F32))
        keep = {
            "x": sb("x", [P, NB, F]), "mean_v": sb("mean_v", [P, F]), "ident": sb("ident", [P, P]),
            "ones": sb("ones", [P, P]), "zeros": sb("zeros", [P, BANK], BF16),
        }
        x = keep["x"]
        s_x, s_c = ctx.enter_context(nc.semaphore("x_in")), ctx.enter_context(nc.semaphore("constants"))
        with nc.Block() as block:
            @block.sync
            def _(sp):
                sp.dma_start(x[:], a["x"].rearrange("(b p) f -> p b f", p=P)).then_inc(s_x, 16)
                sp.dma_start(keep["ident"][:], a["ident"]).then_inc(s_x, 16)
                sp.wait_ge(s_x, 32)

            @block.vector
            def _(dve):
                dve.memset(keep["ones"][:], 1.0 / N).then_inc(s_c, 1)
                dve.memset(keep["zeros"][:], 0.0).then_inc(s_c, 1)
                dve.wait_ge(s_c, 2)
        w1a, w1b = a["W1"], a["W2"]
        less_1 = dram("less_1", [N, N])
        if "0" in layers:
            l0 = dict(name="l0", nh=1, d=F, src=x, norm=True, w=a["eye"], jvec=a["a0"][F:2 * F, 0], ivec=a["a0"][0:F, 0],
                      aux=dram("aux0", [NB, P, F + 2]), irow=dram("irow0", [NB, 1, P]), elu=False, mean=True)
            phase(prepare, "p0", l0)
            phase(attend, "l0", l0, a["adj_t"])
        if "1" in layers:
            with nc.sbuf_tensor("h1", [P, NB, F], F32) as h1:
                for name, src, w, av, dst in (("l1a", x, w1a, a["a1"], h1), ("l1b", h1, w1b, a["a2"], None)):
                    l1 = dict(name=name, nh=4, d=64, src=src, norm=dst is not None, w=w, jvec=av[1], ivec=av[0],
                              aux=dram("aux" + name, [NB, P, F + 8]), irow=dram("irow" + name, [NB, 4, P]),
                              elu=True, mean=True, dst=dst,
                              mask={"adj": a["adj"], "less_1": less_1, "first": 0 if dst is not None else NB // 2})
                    phase(prepare, "p" + name, l1)
                    phase(attend, name, l1, a["adj_t"])
        if "2" in layers:
            l2 = dict(name="l2", nh=8, d=32, src=x, norm=True, w=a["w2"], jvec=a["ar2"], ivec=a["al2"],
                      aux=dram("aux2", [NB, P, F + 16]), irow=dram("irow2", [NB, 8, P]), elu=False, mean=True,
                      pair={"curv": a["curv"], "wc": a["wc"], "gate": a["gate"], "brow": dram("brow2", [NB, 8, P]),
                            "curv_t": a["curv_t"], "wc_t": a["wc_t"], "curv_g": a["curv_g"], "same_i": a["same_i"],
                            "krow": dram("krow2", [NB, 8, P]), "x_rows": dram("x_rows", [N, F]),
                            "less_1": less_1})
            phase(prepare, "p2", l2)
            phase(attend_pairwise, "l2", l2)
        if "3" in layers:
            l3 = dict(name="l3", nh=4, d=64, src=x, norm=True, w=a["w3"], jvec=a["u3"], ivec=a["v3"],
                      aux=dram("aux3", [NB, P, F + 8]), irow=dram("irow3", [NB, 4, P]),
                      elu=False, mean=False, nonzero=True, proj={"w": a["pw3"], "bias": [a["b3"], a["pb3"]]})
            phase(prepare, "p3", l3)
            phase(attend, "l3", l3, a["adj_t"])
        s_o = ctx.enter_context(nc.semaphore("out_written"))
        with nc.Block() as block:
            @block.sync
            def _(sp):
                sp.dma_start(out.rearrange("(b p) f -> p b f", p=P), x[:]).then_inc(s_o, 16)
                sp.wait_ge(s_o, 16)


LAYERS = "0123"


def kernel(**inputs):
    import numpy as _np
    import concourse.bacc as _bacc
    from concourse import mybir as _mybir
    from concourse.bass_utils import run_bass_kernel_spmd as _run

    i = {k: _np.asarray(v) for k, v in inputs.items()}
    heads = lambda w: w.transpose(1, 0, 2).reshape(F, F)
    halves = lambda v: v.reshape(4, 2, 64).transpose(1, 0, 2).reshape(2, F)
    same_i = _np.zeros((KM - 1, NH2, R), _np.float32)
    for r in range(R):
        same_i[r:KD:R, :, r] = 1.0
        same_i[KD + r, :, r] = BIG
    for h in range(NH2):
        same_i[KD + R + h, h, :] = 1.0
    curv = i["L2_gnn_curv_feats"]
    put = {
        "adj": i["adj"], "w2": i["L2_gnn_W"].T, "al2": i["L2_gnn_a_l"].reshape(F), "ar2": i["L2_gnn_a_r"].reshape(F),
        "curv": curv, "curv_t": curv.T, "curv_g": curv.reshape(GN, R, NF).transpose(2, 1, 0).reshape(KD, GN),
        "wc": i["L2_gnn_Wc"], "wc_t": i["L2_gnn_Wc"].T, "gate": i["L2_gnn_gate"].reshape(1),
        "same_i": same_i.reshape(KM - 1, P),
        "x": i["x"], "adj_t": i["adj"].T, "a0": i["L0_gnn_a"],
        "W1": heads(i["L1_gnn_W1"]), "a1": halves(i["L1_gnn_a1"]),
        "W2": heads(i["L1_gnn_W2"]), "a2": halves(i["L1_gnn_a2"]),
        "w3": i["L3_gnn_weight"], "u3": i["L3_gnn_weight_u"].reshape(F), "v3": i["L3_gnn_weight_v"].reshape(F),
        "b3": i["L3_gnn_bias"].reshape(F), "pb3": i["L3_gnn_proj_b"], "pw3": i["L3_gnn_proj_w"].T,
        "ident": _np.eye(P, dtype=_np.float32), "eye": _np.eye(F, dtype=_np.float32),
    }
    nc = _bacc.Bacc("TRN2", target_bir_lowering=False, num_devices=1)
    arrays, aps = {}, {}
    for name, v in put.items():
        v = _np.ascontiguousarray(v)
        arrays[name + "_dram"] = v
        aps[name] = nc.dram_tensor(name + "_dram", v.shape, _mybir.dt.from_np(v.dtype), kind="ExternalInput").ap()
    o = nc.dram_tensor("out_dram", (N, F), F32, kind="ExternalOutput").ap()
    build(nc, aps, o, LAYERS)
    r = _run(nc, [arrays], core_ids=[0])
    return r.results[0]["out_dram"]
```

```python
from contextlib import ExitStack

import concourse.bass as bass
from concourse import mybir

F32 = mybir.dt.float32
I32 = mybir.dt.int32
I16 = mybir.dt.int16
BF16 = mybir.dt.bfloat16
ALU = mybir.AluOpType
ACT = mybir.ActivationFunctionType
AX = mybir.AxisListType
RMAX = bass.bass_isa.ReduceOp.max

N = 4096
F = 256
P = 128
NB = N // P
KC = F // P
BANK = 512
EPS = 1e-5
SLOPE = 0.2
POS = 1.0 - SLOPE
CAP = 70.0
IT = 1024
NIT = N // IT
IB = IT // P
UN = 8
NF = 6
R = 16
GN = N // R
IT2 = BANK
NIT2 = N // IT2
G2 = IT2 // R
JP = 256
NH2 = 8
KD = NF * R
KM = KD + R + NH2 + 1
BIG = 1e9
SHIFT = 60.0


def chained(eng, sem):
    count = [0]

    def run(ins):
        count[0] += 1
        ins.then_inc(sem, 1)
        eng.wait_ge(sem, count[0])
    return run


def prepare(nc, sem, ps, keep, layer):
    name, nh, d, src, norm = layer["name"], layer["nh"], layer["d"], layer["src"], layer["norm"]
    C = F + 2 * nh
    proj = layer.get("proj")
    x, mean_v, ident, ones = keep["x"], keep["mean_v"], keep["ident"], keep["ones"]
    s_w, s_vec = sem("weights_in"), sem("vectors_in")
    s_wcat, s_link = sem("weights_ready"), sem("prep_chain")
    s_st, s_var, s_std, s_rstd = sem("row_stats"), sem("variance"), sem("deviation"), sem("rstd")
    s_h, s_t, s_tc, s_p, s_hs = sem("rows"), sem("turned_psum"), sem("turned"), sem("projected"), sem("kept")
    s_pm, s_M, s_dq, s_q, s_one = sem("part_max"), sem("max_all"), sem("shifted"), sem("q"), sem("ones_set")
    s_vs, s_vm, s_fi, s_ft, s_fit = sem("value_sums"), sem("mean_psum"), sem("fi"), sem("fi_psum"), sem("fi_rows")
    s_vp = sem("value_part_sums")
    s_out, s_xa = sem("prep_out"), sem("x_added")
    pair = layer.get("pair")
    s_pc, s_cM, s_rt, s_rrow = sem("curv_part_max"), sem("curv_max"), sem("bound"), sem("bound_rows")
    e = d + 1 if pair else d
    CA = nh * e

    def values(t):
        return t.rearrange("p b (h e) -> p b h e", e=e)[:, :, :, 0:d]
    FK = max(1, nh * NB // P)
    FR = min(P, nh * NB)
    with ExitStack() as ctx:
        def sb(what, shape):
            return ctx.enter_context(nc.sbuf_tensor(f"{name}_{what}", shape, F32))
        hs = sb("hs", [P, NB, CA])
        ij = sb("ij", [P, NB, 2 * nh])
        wcat = sb("wcat", [P, KC, C])
        vecs = sb("vecs", [P, 2, F])
        wtmp = sb("wtmp", [P, KC, F])
        rows = sb("rows", [P, 4, F])
        turned = sb("turned", [P, 2, F])
        st = sb("st", [P, NB, 6])
        sm = sb("sm", [P, 6, NB])
        pm = sb("pm", [P, nh])
        M = sb("M", [P, nh])
        cap = sb("cap", [P, nh])
        shifted = sb("shifted", [P, NB, nh])
        vparts = sb("vparts", [P, NB // 4, CA])
        vsum = sb("vsum", [P, CA])
        fi = sb("fi", [P, NB, nh])
        fit = sb("fit", [P, FK, P])
        if proj:
            wproj = sb("wproj", [P, KC, F])
            pbias = sb("pbias", [P, 2, F])
        if pair:
            curv = sb("curv", [P, NB, NF])
            cmax = sb("cmax", [P, 2, NF])
            gw = sb("gw", [P, nh, NF])
            gate = sb("gate", [P, 1])
            far = sb("far", [P, 2, NB * NF])
            prod = sb("prod", [P, NB, nh * NF])
            bound = sb("bound", [P, 3, NB * nh])
            boundt = sb("boundt", [P, 2 * FK, P])
            wrow = sb("wrow", [P, nh, NF])
        rstd, shift = sm[:, 4, :], sm[:, 5, :]
        REST = (NB - NB // 4) // 4
        ranges = (slice(0, NB // 4), slice(NB // 4, NB))
        fj_raw, fi_raw = ij[:, :, 0:nh], ij[:, :, nh:2 * nh]
        pos_fj, q, fj_less = (keep["j_part"][:, k, :, 0:nh] for k in range(3))
        block = ctx.enter_context(nc.Block())

        @block.sync
        def _(sp):
            for c in range(KC):
                sp.dma_start(wcat[:, c, 0:F], layer["w"][c * P:(c + 1) * P, :]).then_inc(s_w, 16)
            if pair:
                sp.dma_start(pair["x_rows"].rearrange("(b p) f -> p b f", p=P), x[:]).then_inc(s_out, 16)
            if nh > 1:
                sp.dma_start(vecs[:, 0, :], layer["jvec"].partition_broadcast(P)).then_inc(s_vec, 16)
                sp.dma_start(vecs[:, 1, :], layer["ivec"].partition_broadcast(P)).then_inc(s_vec, 16)
            else:
                for c in range(KC):
                    for col, vec in ((F, "jvec"), (F + 1, "ivec")):
                        sp.dma_start(wcat[:, c, col:col + 1],
                                     layer[vec][c * P:(c + 1) * P].unsqueeze(1)).then_inc(s_vec, 16)
            if proj:
                sp.dma_start(wproj[:], proj["w"].rearrange("(c p) n -> p c n", p=P)).then_inc(s_w, 16)
                for k in range(2):
                    sp.dma_start(pbias[:, k, :], proj["bias"][k].partition_broadcast(P)).then_inc(s_vec, 16)
            if pair:
                sp.dma_start(curv[:], pair["curv"].rearrange("(b p) f -> p b f", p=P)).then_inc(s_vec, 16)
                sp.dma_start(gw[:].rearrange("p h f -> p (h f)"),
                             pair["wc"].rearrange("h f -> (h f)").partition_broadcast(P)).then_inc(s_vec, 16)
                sp.dma_start(gate[:], pair["gate"].partition_broadcast(P)).then_inc(s_vec, 16)
            for k in range(4):
                part = slice(k * NB // 4, (k + 1) * NB // 4)
                sp.wait_ge(s_hs, 2 * ((k + 1) * NB // 4) + 4)
                if pair:
                    sp.wait_ge(s_one, 1)
                sp.dma_start(layer["aux"][part].rearrange("b p c -> p b c"), hs[:, part, :]).then_inc(s_out, 16)
            sp.wait_ge(s_fit, FK)
            irow = layer["irow"].rearrange("b h n -> (b h) n")
            for k in range(FK):
                sp.dma_start(irow[k * FR:(k + 1) * FR, :], fit[0:FR, k, :]).then_inc(s_out, 16)
            if pair:
                sp.wait_ge(s_rrow, 2 * FK)
                brow = pair["brow"].rearrange("b h n -> (b h) n")
                krow = pair["krow"].rearrange("b h n -> (b h) n")
                for k in range(FK):
                    sp.dma_start(brow[k * P:(k + 1) * P, :], boundt[:, k, :]).then_inc(s_out, 16)
                    sp.dma_start(krow[k * P:(k + 1) * P, :], boundt[:, FK + k, :]).then_inc(s_out, 16)
                sp.wait_ge(s_out, 16 + 16 * 4 + 48 * FK)
            else:
                sp.wait_ge(s_out, 16 * 4 + 16 * FK)

        @block.gpsimd
        def _(pool):
            pool.wait_ge(s_pm, 1)
            pool.partition_all_reduce(M[:], pm[:], P, RMAX).then_inc(s_M, 1)
            if pair:
                pool.wait_ge(s_pc, 1)
                pool.partition_all_reduce(cmax[:], cmax[:], P, RMAX).then_inc(s_cM, 1)

        @block.scalar
        def _(act):
            def deviations(k):
                if norm:
                    b = ranges[k]
                    act.wait_ge(s_var, k + 1)
                    act.activation(sm[:, 3, b], sm[:, 2, b], ACT.Sqrt).then_inc(s_std, 1)
                    act.wait_ge(s_rstd, k + 1)

            def normalise(b, k):
                act.wait_ge(s_t, b + 1)
                row = src[:, bass.ds(b, 1), :].rearrange("p a c -> p (a c)")
                if norm:
                    act.activation(rows[:, k, :], row, ACT.Relu, bias=shift[:, bass.ds(b, 1)],
                                   scale=rstd[:, bass.ds(b, 1)]).then_inc(s_h, 1)
                else:
                    act.copy(rows[:, k, :], row).then_inc(s_h, 1)

            def turn(t, last):
                for k in range(4):
                    if k < 2 or not last:
                        normalise(t * 4 + k + 2, (k + 2) % 4)
                    act.wait_ge(s_p, t * 4 + k + 3)
                    b = t * 4 + k
                    act.copy(values(hs[:, bass.ds(b, 1), :]).rearrange("p a h d -> p (a h) d"),
                             ps[:, 2 + k % 2, 0:F].rearrange("p (h d) -> p h d", d=d)).then_inc(s_hs, 1)
                    act.copy(ij[:, bass.ds(b, 1), :].rearrange("p a c -> p (a c)"),
                             ps[:, 2 + k % 2, F:C]).then_inc(s_hs, 1)

            deviations(0)
            normalise(0, 0)
            normalise(1, 1)
            turn(0, False)
            deviations(1)
            with act.Fori(1, NB // 4 - 1) as t:
                turn(t, False)
            turn(NB // 4 - 1, True)
            act.wait_ge(s_dq, 1)
            act.activation(q, shifted[:], ACT.Exp, scale=SLOPE).then_inc(s_q, 1)

        @block.tensor
        def _(pe):
            pe.sem_inc(s_t, 4)
            pe.sem_inc(s_p, 2)

            def transpose_rows(b, k):
                pe.wait_ge(s_h, b + 1)
                for c in range(KC):
                    ins = pe.transpose(ps[:, k % 2, c * P:(c + 1) * P], rows[:, k, c * P:(c + 1) * P], ident[:])
                ins.then_inc(s_t, 1)

            def turn(t, last):
                for k in range(4):
                    if k < 3 or not last:
                        transpose_rows(t * 4 + k + 1, (k + 1) % 4)
                    pe.wait_ge(s_tc, t * 4 + k + 1)
                    pe.wait_ge(s_hs, (t * 4 + k) * 2 + 2)
                    for c in range(KC):
                        ins = pe.matmul(ps[:, 2 + k % 2, 0:C], turned[:, k % 2, c * P:(c + 1) * P], wcat[:, c, :],
                                        start=c == 0, stop=c == KC - 1)
                    if proj:
                        pe.wait_ge(s_xa, t * 4 + k + 1)
                        for c in range(KC):
                            ins = pe.matmul(ps[:, 4 + k % 2, 0:F], turned[:, k % 2, c * P:(c + 1) * P], wproj[:, c, :],
                                            start=c == 0, stop=c == KC - 1)
                    ins.then_inc(s_p, 1)

            transpose_rows(0, 0)
            pe.wait_ge(s_w, 16 * KC + (16 if proj else 0))
            pe.wait_ge(s_wcat, 1)
            with pe.Fori(0, NB // 4 - 1) as t:
                turn(t, False)
            turn(NB // 4 - 1, True)
            pe.wait_ge(s_fi, 1)
            flat = fi[:].rearrange("p b h -> p (b h)")
            for k in range(FK):
                pe.transpose(ps[0:FR, 7, k * P:(k + 1) * P], flat[:, k * FR:(k + 1) * FR], ident[:]).then_inc(s_ft, 1)
            if pair:
                pe.wait_ge(s_rt, 1)
                for r in range(2):
                    for k in range(FK):
                        pe.transpose(ps[:, 5, (r * FK + k) * P:(r * FK + k + 1) * P],
                                     bound[:, r, k * P:(k + 1) * P], ident[:]).then_inc(s_ft, 1)
            if layer["mean"]:
                pe.wait_ge(s_vs, 1)
                pe.matmul(ps[:, 6, 0:CA], ones[:], vsum[:], start=True, stop=True).then_inc(s_vm, 1)

        @block.vector
        def _(dve):
            link = chained(dve, s_link)
            if pair:
                dve.memset(hs[:].rearrange("p b (h e) -> p b h e", e=e)[:, :, :, d], 1.0).then_inc(s_one, 1)
            dve.sem_inc(s_hs, 4)
            dve.sem_inc(s_xa, 2)
            def loaded(k):
                if "loads" in layer:
                    dve.wait_ge(layer["loads"][k], 16)

            def stats(b):
                dve.bn_stats(st[:, bass.ds(b, 1), :].rearrange("p a c -> p (a c)"),
                             src[:, bass.ds(b, 1), :].rearrange("p a c -> p (a c)")).then_inc(s_st, 1)

            def rstds(k):
                b = ranges[k]
                dve.wait_ge(s_st, b.stop)
                link(dve.tensor_tensor(sm[:, 0, b], st[:, b, 1], st[:, b, 4], ALU.add))
                link(dve.tensor_tensor(sm[:, 1, b], st[:, b, 1], st[:, b, 4], ALU.subtract))
                link(dve.tensor_tensor(sm[:, 1, b], sm[:, 1, b], sm[:, 1, b], ALU.mult))
                link(dve.tensor_tensor(sm[:, 2, b], st[:, b, 2], st[:, b, 5], ALU.add))
                link(dve.scalar_tensor_tensor(sm[:, 2, b], sm[:, 1, b], F / 4.0, sm[:, 2, b], ALU.mult, ALU.add))
                dve.tensor_scalar(sm[:, 2, b], sm[:, 2, b], 1.0 / F, EPS, ALU.mult, ALU.add).then_inc(s_var, 1)
                dve.wait_ge(s_std, k + 1)
                link(dve.reciprocal(sm[:, 4, b], sm[:, 3, b]))
                dve.scalar_tensor_tensor(sm[:, 5, b], sm[:, 0, b], -0.5, sm[:, 4, b], ALU.mult, ALU.mult).then_inc(s_rstd, 1)

            if norm:
                loaded(0)
                with dve.Fori(0, NB // 4) as b:
                    stats(b)
                rstds(0)
            if nh > 1:
                dve.wait_ge(s_w, 16 * KC)
                dve.wait_ge(s_vec, 64 if proj else 80 if pair else 32)
                for k in range(2):
                    w4 = wtmp[:].rearrange("p c (h d) -> p c h d", d=d)
                    wv = wcat[:, :, 0:F].rearrange("p c (h d) -> p c h d", d=d)
                    link(dve.tensor_tensor(w4, wv, vecs[:, k, :].rearrange("p (h d) -> p h d", d=d)
                                           .unsqueeze(1).broadcast_to([P, KC, nh, d]), ALU.mult))
                    link(dve.tensor_reduce(wcat[:, :, F + k * nh:F + (k + 1) * nh], w4, AX.X, ALU.add))
                if proj:
                    link(dve.tensor_tensor(pbias[:, 0, :], pbias[:, 0, :], pbias[:, 1, :], ALU.add))
            else:
                dve.wait_ge(s_vec, 16 * 2 * KC)
            dve.nop().then_inc(s_wcat, 1)

            def copy_turned(b, k):
                dve.wait_ge(s_t, b + 5)
                dve.wait_ge(s_p, b + 1)
                dve.tensor_copy(turned[:, k % 2, :], ps[:, k % 2, 0:F]).then_inc(s_tc, 1)

            def turn(t, last, more_stats=False):
                for k in range(4):
                    if k < 3 or not last:
                        copy_turned(t * 4 + k + 1, k + 1)
                    if more_stats:
                        if k < 3:
                            loaded(k + 1)
                        for b in range(REST):
                            stats(NB // 4 + k * REST + b)
                    if proj:
                        dve.wait_ge(s_p, t * 4 + k + 3)
                        xb = x[:, bass.ds(t * 4 + k, 1), :].rearrange("p a c -> p (a c)")
                        dve.tensor_tensor(xb, xb, ps[:, 4 + k % 2, 0:F], ALU.add).then_inc(s_xa, 1)

            def sum_values(t):
                if layer["mean"]:
                    dve.wait_ge(s_hs, t * 8 + 12)
                    dve.tensor_reduce(vparts[:, bass.ds(t, 1), :].rearrange("p a c -> p (a c)"),
                                      hs[:, bass.ds(t * 4, 4), :].rearrange("p b c -> p c b"),
                                      AX.X, ALU.add).then_inc(s_vp, 1)

            copy_turned(0, 0)
            turn(0, False, more_stats=norm)
            if norm:
                rstds(1)
            with dve.Fori(1, NB // 4 - 1) as t:
                turn(t, False)
                sum_values(t - 1)
            turn(NB // 4 - 1, True)
            dve.wait_ge(s_hs, 2 * NB + 4)
            if proj:
                dve.wait_ge(s_xa, NB + 2)
                link(dve.tensor_tensor(x[:], x[:], pbias[:, 0, :].unsqueeze(1).broadcast_to([P, NB, F]), ALU.add))
            dve.tensor_reduce(pm[:], fj_raw.rearrange("p b c -> p c b"), AX.X, ALU.max).then_inc(s_pm, 1)
            link(dve.tensor_scalar(pos_fj, fj_raw, POS, None, ALU.mult))
            dve.wait_ge(s_M, 1)
            all_M = M[:].unsqueeze(1).broadcast_to([P, NB, nh])
            dve.tensor_tensor(shifted[:], fj_raw, all_M, ALU.subtract).then_inc(s_dq, 1)
            if pair:
                link(dve.memset(cap[:], 3e38))
            else:
                link(dve.tensor_scalar(cap[:], M[:], -POS, CAP, ALU.mult, ALU.add))
            dve.scalar_tensor_tensor(fi[:], fi_raw, POS, cap[:].unsqueeze(1).broadcast_to([P, NB, nh]),
                                     ALU.mult, ALU.min).then_inc(s_fi, 1)
            link(dve.scalar_tensor_tensor(fj_less, all_M, -SLOPE, fj_raw, ALU.mult, ALU.add))
            if pair:
                link(dve.tensor_scalar(far[:, 0, :], curv[:].rearrange("p b f -> p (b f)"), -1.0, None, ALU.mult))
                link(dve.tensor_reduce(cmax[:, 0, :], curv[:].rearrange("p b f -> p f b"), AX.X, ALU.max))
                dve.tensor_reduce(cmax[:, 1, :], far[:, 0, :].rearrange("p (b f) -> p f b", f=NF),
                                  AX.X, ALU.max).then_inc(s_pc, 1)
                link(dve.tensor_scalar(wrow[:], gw[:], gate[:, 0:1], None, ALU.mult))
                link(dve.tensor_scalar(gw[:], wrow[:], 0.0, None, ALU.max))
                dve.wait_ge(s_cM, 1)
                f0 = far[:, 0, :].rearrange("p (b f) -> p b f", f=NF)
                f1 = far[:, 1, :].rearrange("p (b f) -> p b f", f=NF)
                link(dve.tensor_tensor(f0, f0, cmax[:, 0:1, :].broadcast_to([P, NB, NF]), ALU.add))
                link(dve.tensor_tensor(f1, curv[:], cmax[:, 1:2, :].broadcast_to([P, NB, NF]), ALU.add))
                link(dve.tensor_tensor(f0, f0, f1, ALU.max))
                pr = prod[:].rearrange("p b (h f) -> p b h f", f=NF)
                link(dve.tensor_tensor(pr, f0.unsqueeze(2).broadcast_to([P, NB, nh, NF]),
                                       gw[:].unsqueeze(1).broadcast_to([P, NB, nh, NF]), ALU.mult))
                b3 = [bound[:, k, :].rearrange("p (b h) -> p b h", h=nh) for k in range(3)]
                link(dve.tensor_reduce(b3[1], pr, AX.X, ALU.add))
                link(dve.tensor_tensor(b3[2], fi_raw, all_M, ALU.add))
                link(dve.tensor_scalar(bound[:, 2, :], bound[:, 2, :], 0.0, -POS, ALU.max, ALU.mult))
                link(dve.tensor_tensor(bound[:, 0, :], bound[:, 2, :], bound[:, 1, :], ALU.subtract))
                link(dve.tensor_tensor(pr, curv[:].unsqueeze(2).broadcast_to([P, NB, nh, NF]),
                                       wrow[:].unsqueeze(1).broadcast_to([P, NB, nh, NF]), ALU.mult))
                link(dve.tensor_reduce(b3[2], pr, AX.X, ALU.add))
                link(dve.scalar_tensor_tensor(b3[1], shifted[:], SLOPE, b3[2], ALU.mult, ALU.subtract))
                link(dve.scalar_tensor_tensor(bound[:, 0, :], bound[:, 0, :], SHIFT, bound[:, 2, :], ALU.add, ALU.add))
                dve.nop().then_inc(s_rt, 1)
            dve.wait_ge(s_ft, FK)
            for k in range(FK):
                dve.tensor_copy(fit[0:FR, k, :], ps[0:FR, 7, k * P:(k + 1) * P]).then_inc(s_fit, 1)
            if pair:
                dve.wait_ge(s_ft, 3 * FK)
                for k in range(2 * FK):
                    dve.tensor_copy(boundt[:, k, :], ps[:, 5, k * P:(k + 1) * P]).then_inc(s_rrow, 1)
            if layer["mean"]:
                sum_values(NB // 4 - 2)
                sum_values(NB // 4 - 1)
                dve.wait_ge(s_vp, NB // 4)
                dve.tensor_reduce(vsum[:], vparts[:].rearrange("p b c -> p c b"), AX.X, ALU.add).then_inc(s_vs, 1)
                dve.wait_ge(s_vm, 1)
                link(dve.tensor_copy(mean_v[:].rearrange("p (h d) -> p h d", d=d),
                                     ps[:, 6, 0:CA].rearrange("p (h e) -> p h e", e=e)[:, :, 0:d]))


def finisher(dve, ps, keep, layer, it, bufs, sems):
    nh, elu, dst = layer["nh"], layer["elu"], layer.get("dst")
    den, att, tmp = bufs
    s_link, s_ot, s_post, s_mn, s_e, s_dt = sems
    TB = IB // 2
    d = F // nh
    links = 3 + TB * (1 + 2 * bool(layer["mean"]) + elu * (2 if dst is None else 1))
    count = [0]

    def link(ins):
        count[0] += 1
        ins.then_inc(s_link, 1)
        dve.wait_ge(s_link, it * links + count[0])

    def sums():
        dve.wait_ge(s_dt, it + 1)
        turned = ps[:, 6, 0:4 * IB]
        if nh > 1:
            ins = dve.tensor_copy(den[:, 0].rearrange("p b h -> p (b h)"), turned)
        else:
            ins = dve.tensor_reduce(den[:, 0].rearrange("p b h -> p (b h)"),
                                    turned.rearrange("p (b g) -> p b g", g=4), AX.X, ALU.add)
        ins.then_inc(s_post, 1)
        dve.wait_ge(s_post, it * (TB + 1) + 2)
        link(dve.tensor_scalar(den[:, 1], den[:, 0], 0.0, None, ALU.is_equal))
        link(dve.tensor_tensor(den[:, 2], den[:, 0], den[:, 1], ALU.add))
        link(dve.reciprocal(den[:, 3], den[:, 2]))
    wide = [P, 2, nh, d]
    a4 = att[:].rearrange("p b (h d) -> p b h d", h=nh)
    t4 = tmp[:].rearrange("p b (h d) -> p b h d", h=nh)
    m4 = keep["mean_v"][:].rearrange("p (h d) -> p h d", h=nh).unsqueeze(1).broadcast_to(wide)

    def blocks(r):
        dve.wait_ge(s_ot, it * TB + r + 1)
        o = ps[:, 7 - r % 2, :].rearrange("p (b h d) -> p b h d", b=2, h=nh)
        rec = den[:, 3, 2 * r:2 * r + 2, :].unsqueeze(3).broadcast_to(wide)
        dve.tensor_tensor(a4, o, rec, ALU.mult).then_inc(s_post, 1)
        if layer["mean"]:
            none = den[:, 1, 2 * r:2 * r + 2, :].unsqueeze(3).broadcast_to(wide)
            link(dve.tensor_tensor(t4, m4, none, ALU.mult))
        dve.wait_ge(s_post, it * (TB + 1) + r + 3)
        if layer["mean"]:
            link(dve.tensor_tensor(att[:], att[:], tmp[:], ALU.add))
        rows = (dst if dst is not None else keep["x"])[:, bass.ds(it * IB + 2 * r, 2), :]
        if elu:
            dve.tensor_scalar(tmp[:], att[:], 0.0, None, ALU.min).then_inc(s_mn, 1)
            link(dve.tensor_scalar(att[:], att[:], 0.0, -1.0, ALU.max, ALU.add))
            dve.wait_ge(s_e, it * TB + r + 1)
            if dst is None:
                link(dve.tensor_tensor(att[:], att[:], tmp[:], ALU.add))
                link(dve.tensor_tensor(rows, rows, att[:], ALU.add))
            else:
                link(dve.tensor_tensor(rows, att[:], tmp[:], ALU.add))
        else:
            link(dve.tensor_tensor(rows, rows, att[:], ALU.add))
        assert count[0] == links or r < TB - 1, (count[0], links)
    return sums, blocks


def attend(nc, sem, ps, keep, layer, adj_t):
    name, nh, elu = layer["name"], layer["nh"], layer["elu"]
    ident, zeros = keep["ident"], keep["zeros"]
    mask, nonzero = layer.get("mask"), layer.get("nonzero")
    RING = 4 if nh > 1 else 8
    WB = 8 // nh
    NT = NB // UN
    US = 8 if nonzero else 4
    finish_after = ((1, 2), (3, 4), (5, 6), (7,))
    DEN = 4
    TB = IB // 2
    s_in = [sem(f"tile_in{k}") for k in range(RING)]
    s_fi = [sem(f"fi_in{h}") for h in range(nh)]
    s_u, s_p, s_pv = sem("exps"), sem("weights"), sem("contracted")
    s_acc, s_ev, s_dt, s_ot, s_post = sem("tile_done"), sem("evacuated"), sem("sums_turned"), sem("outs_turned"), sem("outs_used")
    s_link, s_mn, s_e = sem("post_chain"), sem("negatives"), sem("elu_exp")
    s_sign, s_a16, s_ed = sem("signs"), sem("adj_16_bits"), sem("edges")
    s_ri, s_rc, s_ro = sem("adj_rows_in"), sem("adj_rows_less_1"), sem("adj_rows_out")
    s_rf = sem("adj_rows_free")
    s_ws, s_summed = sem("weights_added"), sem("added_weights_summed")
    with ExitStack() as ctx:
        def sb(what, shape, dt=F32):
            return ctx.enter_context(nc.sbuf_tensor(f"{name}_att_{what}", shape, dt))
        fi = sb("fi", [P, nh, IT])
        adj = sb("adj", [P, RING, IT], I32)
        aux = sb("aux", [P, RING, F])
        u = sb("u", [P, US, IT])
        w = sb("w", [P, 8, IT])
        ot = sb("ot", [P, 6, BANK])
        den = sb("den", [P, 4, IB, nh])
        att = sb("att", [P, 2, F])
        tmp = sb("tmp", [P, 2, F])
        if nonzero:
            edges = sb("edges", [P, US, IT], I16)
            adj16 = sb("adj16", [P, 2, IT], I16)
        if nh == 1:
            wsum = sb("wsum", [P, 4, IT])
        if mask:
            arows = sb("arows", [P, N], I32)
        pos_fj, q, fj_less = (keep["j_part"][:, k] for k in range(3))
        block = ctx.enter_context(nc.Block())

        @block.sync
        def _(sp):
            with sp.Fori(0, NIT) as it:
                with sp.Fori(0, NB // UN) as t:
                    for k in range(UN):
                        j = t * UN + k
                        g = it * NB + j
                        if mask and k == 3:
                            row = it * (NB // UN) + t
                            sp.wait_ge(s_rf, row + 1)
                            sp.dma_start(arows[:], mask["adj"][bass.ds(row * P + mask["first"] * P, P), :]
                                         ).then_inc(s_ri, 16)
                        sp.wait_ge(s_pv, g + 1)
                        sp.dma_start(adj[:, k % RING, :],
                                     adj_t[bass.ds(j * P, P), bass.ds(it * IT, IT)]).then_inc(s_in[k % RING], 16)
                        sp.dma_start(aux[:, k % RING, :],
                                     layer["aux"][bass.ds(j, 1), :, :].rearrange("a p c -> (a p) c")
                                     ).then_inc(s_in[k % RING], 16)

        @block.scalar
        def _(act):
            def fi_in(it, h):
                act.dma_start(fi[:, h, :].rearrange("p (b n) -> p b n", n=P),
                              layer["irow"][bass.ds(it * IB, IB), h, :].partition_broadcast(P)).then_inc(s_fi[h], 16)

            def exps(it, t, k, new=False, reload=False):
                for h in range(nh):
                    n = (it * NB + t * UN + k) * nh + h
                    if new:
                        act.wait_ge(s_fi[h], it * 16 + 16)
                    act.wait_ge(s_p, n + 1)
                    act.activation(u[:, (k * nh + h) % US, :], fi[:, h, :], ACT.Exp,
                                   bias=fj_less[:, bass.ds(t * UN + k, 1), h]).then_inc(s_u, 1)
                    if nonzero:
                        act.activation(edges[:, (k * nh + h) % US, :], fi[:, h, :], ACT.Sign,
                                       bias=pos_fj[:, bass.ds(t * UN + k, 1), h]).then_inc(s_sign, 1)
                    if reload:
                        act.wait_ge(s_sign if nonzero else s_u, n + 1)
                        fi_in(it + 1, h)

            def tile(it, more):
                with act.Fori(1, NT - 1) as t:
                    for k in range(UN):
                        exps(it, t, k)
                for k in range(UN):
                    exps(it, NT - 1, k, reload=more and k == UN - 1)
                if more:
                    exps(it + 1, 0, 0, new=True)
                act.wait_ge(s_acc, it + 1)
                for c in range(3):
                    act.copy(ot[:, c, :], ps[:, c, :]).then_inc(s_ev, 1)
                for r in range(TB):
                    if more:
                        for k in finish_after[r]:
                            exps(it + 1, 0, k)
                    if elu:
                        act.wait_ge(s_mn, it * TB + r + 1)
                        act.activation(tmp[:], tmp[:], ACT.Exp).then_inc(s_e, 1)

            for h in range(nh):
                fi_in(0, h)
            for k in range(UN):
                exps(0, 0, k, new=k == 0)
            with act.Fori(0, NIT - 1) as it:
                tile(it, True)
            tile(NIT - 1, False)

        @block.gpsimd
        def _(pool):
            if mask:
                pool.sem_inc(s_rf, 1)
                with pool.Fori(0, NIT * NB // UN) as row:
                    pool.wait_ge(s_rc, row * 4 + 4)
                    pool.dma_start(mask["less_1"][bass.ds(row * P + mask["first"] * P, P), :],
                                   arows[:].bitcast(F32)).then_inc(s_ro, 16)
                    pool.wait_ge(s_ro, row * 16 + 16)
                    pool.sem_inc(s_rf, 1)

        @block.vector
        def _(dve):
            dve.sem_inc(s_p, US)
            dve.sem_inc(s_post, 1)

            def weights(it, t, k):
                if mask and 2 <= k < 6:
                    if k == 2:
                        dve.wait_ge(s_ri, (it * NT + t) * 16 + 16)
                    piece = arows[:, (k - 2) * IT:(k - 1) * IT]
                    dve.tensor_scalar(piece.bitcast(F32), piece, -1.0, None, ALU.add).then_inc(s_rc, 1)
                dve.wait_ge(s_in[k % RING], (it * (NB // RING) + t * (UN // RING) + k // RING + 1) * 32)
                if nonzero:
                    dve.tensor_copy(adj16[:, k % 2, :], adj[:, k % RING, :]).then_inc(s_a16, 1)
                    dve.wait_ge(s_a16, it * NB + t * UN + k + 1)
                    first = k * nh % US
                    block_edges = edges[:, first:first + nh, :]
                    dve.wait_ge(s_sign, (it * NB + t * UN + k) * nh + nh)
                    dve.tensor_tensor(block_edges, block_edges, adj16[:, k % 2:k % 2 + 1, :].broadcast_to([P, nh, IT]),
                                      ALU.bitwise_and).then_inc(s_ed, 1)
                    dve.wait_ge(s_ed, it * NB + t * UN + k + 1)
                dve.wait_ge(s_pv, it * NB + t * UN + k + 1 + RING - WB)
                for h in range(nh):
                    n = (it * NB + t * UN + k) * nh + h
                    dve.wait_ge(s_u, n + 1)
                    edge = adj[:, k % RING, :]
                    if nonzero:
                        edge = edges[:, first + h, :]
                    dve.scalar_tensor_tensor(w[:, (k * nh + h) % 8, :], u[:, (k * nh + h) % US, :],
                                             q[:, bass.ds(t * UN + k, 1), h], edge, ALU.max, ALU.mult).then_inc(s_p, 1)
                if nh == 1:
                    n = it * NB + t * UN + k
                    dve.wait_ge(s_p, n + 1 + US)
                    if isinstance(t, int) and t == 0 and k < 4:
                        dve.wait_ge(s_summed, it + 1)
                        dve.tensor_copy(wsum[:, k, :], w[:, k, :]).then_inc(s_ws, 1)
                    else:
                        dve.wait_ge(s_ws, n - 3)
                        dve.tensor_tensor(wsum[:, k % 4, :], wsum[:, k % 4, :], w[:, k, :], ALU.add).then_inc(s_ws, 1)

            def tile(it, more):
                with dve.Fori(1, NT) as t:
                    for k in range(UN):
                        weights(it, t, k)
                if more:
                    weights(it + 1, 0, 0)
                dve.wait_ge(s_acc, it + 1)
                for c in range(3, 6):
                    dve.tensor_copy(ot[:, c, :], ps[:, c, :]).then_inc(s_ev, 1)
                sums, blocks = finisher(dve, ps, keep, layer, it, (den, att, tmp),
                                        (s_link, s_ot, s_post, s_mn, s_e, s_dt))
                for r in range(TB):
                    if more:
                        for k in finish_after[r]:
                            weights(it + 1, 0, k)
                            if k == 1:
                                sums()
                    elif r == 0:
                        sums()
                    blocks(r)

            for k in range(UN):
                weights(0, 0, k)
            with dve.Fori(0, NIT - 1) as it:
                tile(it, True)
            tile(NIT - 1, False)

        @block.tensor
        def _(pe):
            pe.sem_inc(s_summed, 1)
            pe.sem_inc(s_pv, RING)

            def sum_weights(parts):
                for c in range(2):
                    for e in range(4):
                        ins = pe.matmul(ps[32 * e:32 * e + 32, DEN + c, :], keep["one_cols"][:],
                                        parts[e][:, c * BANK:(c + 1) * BANK],
                                        start=False, stop=False, skip_group_check=True)
                return ins

            def contract(it, t, k):
                n = (it * NB + t * UN + k) * nh
                a = aux[:, k % RING, :]
                if nh > 1:
                    for pair in range(nh // 2):
                        pe.wait_ge(s_p, n + 2 * pair + 2 + US)
                        for c in range(2):
                            for e in range(2):
                                h = 2 * pair + e
                                pe.matmul(ps[64 * e:64 * e + 64, 2 * pair + c, :], a[:, 64 * h:64 * h + 64],
                                          w[:, (k * nh + h) % 8, c * BANK:(c + 1) * BANK],
                                          start=False, stop=False, skip_group_check=True)
                else:
                    pe.wait_ge(s_p, n + 1 + US)
                    for half in range(2):
                        for c in range(2):
                            ins = pe.matmul(ps[:, 2 * half + c, :], a[:, half * P:(half + 1) * P],
                                      w[:, k, c * BANK:(c + 1) * BANK],
                                      start=False, stop=False, skip_group_check=True)
                if nh > 1:
                    ins = sum_weights([w[:, (k * nh + h) % 8, :] for h in range(nh)])
                ins.then_inc(s_pv, 1)

            def clear():
                for c in range(6):
                    pe.matmul(ps[:, c, :], zeros[:, 0:P], zeros[:], start=True, stop=False, skip_group_check=True)

            def tile(it, more):
                with pe.Fori(1, NT) as t:
                    for k in range(UN):
                        contract(it, t, k)
                if nh == 1:
                    pe.wait_ge(s_ws, it * NB + NB)
                    sum_weights([wsum[:, e, :] for e in range(4)]).then_inc(s_summed, 1)
                for c in range(6):
                    ins = pe.matmul(ps[:, c, :], zeros[:, 0:P], zeros[:], start=False, stop=True, skip_group_check=True)
                ins.then_inc(s_acc, 1)
                pe.wait_ge(s_post, it * (TB + 1) + 1)
                pe.wait_ge(s_ev, it * 6 + 6)
                for b in range(IB):
                    ins = pe.matmul(ps[:, 6, 4 * b:4 * b + 4], ot[:, DEN + b // 4, (b % 4) * P:(b % 4 + 1) * P],
                                    ident[:, 0:P:32], start=True, stop=True)
                ins.then_inc(s_dt, 1)
                if more:
                    clear()
                for r in range(TB):
                    if more:
                        for k in ((0,), (1, 2), (3, 4), (5, 6))[r]:
                            contract(it + 1, 0, k)
                    pe.wait_ge(s_post, it * (TB + 1) + r + 1)
                    for e in range(2):
                        b = 2 * r + e
                        for half in range(2):
                            ins = pe.transpose(ps[:, 7 - r % 2, e * F + half * P:e * F + (half + 1) * P],
                                               ot[:, 2 * half + b // 4, (b % 4) * P:(b % 4 + 1) * P], ident[:])
                    ins.then_inc(s_ot, 1)
                if more:
                    contract(it + 1, 0, UN - 1)

            clear()
            for k in range(UN):
                contract(0, 0, k)
            with pe.Fori(0, NIT - 1) as it:
                tile(it, True)
            tile(NIT - 1, False)


def attend_pairwise(nc, sem, ps, keep, layer):
    name, nh, pair = layer["name"], layer["nh"], layer["pair"]
    x, mean_v, ident, zeros = keep["x"], keep["mean_v"], keep["ident"], keep["zeros"]
    d = F // nh
    TJ = 4
    NT = NB // TJ
    CG = 2 * BANK // P
    NCH = G2 // CG
    IB2 = IT2 // P
    PARTS = 2 * NCH
    PG = G2 // PARTS
    OUT = 4
    s_in = [sem(f"aux_in{k}") for k in range(TJ)]
    s_m = [sem(f"edges_in{k}") for k in range(2)]
    s_fi = [sem(f"fi_in{h}") for h in range(nh)]
    s_read, s_order = sem("fi_read"), sem("shifts_ordered")
    s_c, s_c2, s_one, s_r, s_d, s_l = (sem("constants_in"), sem("coefficients"), sem("ones_in"),
                                            sem("shift_in"), sem("differences"), sem("relus"))
    s_b, s_t, s_e, s_pv = sem("bias_psum"), sem("logits"), sem("weights"), sem("contracted")
    s_acc, s_ev, s_ot, s_post, s_link = (sem("tile_done"), sem("evacuated"), sem("outs_turned"), sem("outs_used"),
                                         sem("post_chain"))
    s_xa = sem("x_rows_added")
    s_copy, s_xi, s_xd, s_xo = sem("coefficient_chain"), sem("x_rows_in"), sem("x_rows_done"), sem("x_rows_out")
    with ExitStack() as ctx:
        def sb(what, shape, dt=F32):
            return ctx.enter_context(nc.sbuf_tensor(f"{name}_att_{what}", shape, dt))
        diff = sb("diff", [P, 2, G2, JP])
        coef = sb("coef", [KM, G2, P])
        cj = sb("cj", [KD, N])
        ci = sb("ci", [KD, GN])
        gwr = sb("gwr", [KD, nh])
        gate = sb("gate", [KD, 1])
        fi = sb("fi", [P, nh, IT2])
        w_own = sb("w", [P, 2, nh, IT2])
        aux = sb("aux", [P, TJ, nh * (d + 1)])
        ot = sb("ot", [P, 4, BANK])
        den = sb("den", [P, 4, IB2, nh])
        att = sb("att", [P, IB2, F])
        xr = sb("xr", [P, IB2, F])
        xw = x[:].rearrange("p (k b) f -> p k (b f)", k=2).rearrange("p k (h n) -> p k h n", h=nh)
        w = [xw[:, 0], xw[:, 1], w_own[:, 0], w_own[:, 1]]
        x_rows = pair["x_rows"].rearrange("(b p) f -> p b f", p=P)
        pos_fj = keep["j_part"][:, 0]
        block = ctx.enter_context(nc.Block())

        @block.sync
        def _(sp):
            for f in range(NF):
                part = slice(f * R, (f + 1) * R)
                sp.dma_start(cj[part, :], pair["curv_t"][f, :].partition_broadcast(R)).then_inc(s_c, 16)
                sp.dma_start(gwr[part, :], pair["wc_t"][f, :].partition_broadcast(R)).then_inc(s_c, 16)
            sp.dma_start(ci[:], pair["curv_g"]).then_inc(s_c, 16)
            sp.dma_start(gate[:], pair["gate"].partition_broadcast(KD)).then_inc(s_c, 16)
            sp.dma_start(coef[0:KD, 0, :], pair["same_i"][0:KD, :]).then_inc(s_c, 16)
            sp.dma_start(coef[KD:KM - 1, :, :], pair["same_i"][KD:KM - 1, :].unsqueeze(1)
                         .broadcast_to([R + nh, G2, P])).then_inc(s_c, 16)
            for h in range(nh):
                sp.dma_start(pair["shifts"].rearrange("t (b g h n) -> (t b) h g n", b=IB2, h=nh, n=R)[:, h],
                             pair["brow"].rearrange("b h (g n) -> b h g n", n=R)[:, h]).then_inc(s_order, 16)
            sp.dma_start(diff[KM - 1:KM, :, :, :].rearrange("p e g j -> p (e g) j"),
                         pair["one_row"].unsqueeze(0)).then_inc(s_one, 16)
            sp.wait_ge(s_order, 16 * nh)

            def slot_in(it, t, k):
                e = k // 2
                if k % 2 == 0:
                    dp = it * (NB // 2) + t * (TJ // 2) + e
                    sp.wait_ge(s_b, dp * (2 * NCH) + 2 * NCH)
                    sp.dma_start(diff[KD:KD + R, e, :, :],
                                 pair["less_1"][bass.ds(it * IT2, IT2), bass.ds(t * (2 * JP) + e * JP, JP)]
                                 .rearrange("(g i) j -> i g j", i=R)).then_inc(s_m[e], 16)
                sp.dma_start(diff[KD + R:KM - 1, e, :, (k % 2) * P:(k % 2 + 1) * P],
                             pair["krow"][bass.ds(t * TJ + k, 1), :, :].rearrange("a h n -> (a h) n")
                             .unsqueeze(1).broadcast_to([nh, G2, P])).then_inc(s_m[e], 16)

            def aux_in(it, t, k):
                sp.wait_ge(s_pv, it * NB + t * TJ + k + 1)
                sp.dma_start(aux[:, k, :], layer["aux"][bass.ds(t * TJ + k, 1), :, :]
                             .rearrange("a p c -> (a p) c")).then_inc(s_in[k], 16)

            with sp.Fori(0, NIT2) as it:
                slot_in(it, 0, 0)
                slot_in(it, 0, 1)
                sp.wait_ge(s_b, it * (NB * NCH) + 16)
                sp.dma_start(coef[KM - 1:KM, :, :].rearrange("p (a g) m -> p a (g m)", a=16),
                             pair["shifts"][bass.ds(it, 1), :].rearrange("a (b c) -> a b c", b=16)).then_inc(s_r, 16)
                aux_in(it, 0, 0)
                aux_in(it, 0, 1)
                for k in (2, 3):
                    slot_in(it, 0, k)
                    aux_in(it, 0, k)
                sp.wait_ge(s_xd, it + 1)
                sp.dma_start(xr[:], x_rows[:, bass.ds(it * IB2, IB2), :]).then_inc(s_xi, 16)
                with sp.Fori(1, NT) as t:
                    for k in range(TJ):
                        slot_in(it, t, k)
                        aux_in(it, t, k)
            sp.wait_ge(s_xo, 16 * NIT2)
            sp.dma_start(x[:], x_rows).then_inc(s_xi, 16)
            sp.wait_ge(s_xi, 16 * NIT2 + 16)

        @block.gpsimd
        def _(pool):
            pool.sem_inc(s_xd, 1)
            with pool.Fori(0, NIT2) as it:
                pool.wait_ge(s_xa, it * 2 + 2)
                pool.dma_start(x_rows[:, bass.ds(it * IB2, IB2), :], xr[:]).then_inc(s_xo, 16)
                pool.wait_ge(s_xo, it * 16 + 16)
                pool.sem_inc(s_xd, 1)

        @block.scalar
        def _(act):
            def fi_in(it, h):
                act.dma_start(fi[:, h, :].rearrange("p (b n) -> p b n", n=P),
                              layer["irow"][bass.ds(it * IB2, IB2), h, :].partition_broadcast(P)).then_inc(s_fi[h], 16)

            def relus(it, t, k, new=False, reload=False):
                act.wait_ge(s_in[k], (it * NT + t) * 16 + 16)
                for h in range(nh):
                    if new:
                        act.wait_ge(s_fi[h], it * 16 + 16)
                    ins = act.activation(w[k][:, h, :], fi[:, h, :], ACT.Relu, bias=pos_fj[:, bass.ds(t * TJ + k, 1), h])
                    if reload and h < nh - 1:
                        ins.then_inc(s_read, 1)
                        if h > 0:
                            act.wait_ge(s_read, it * (nh - 1) + h)
                            fi_in(it + 1, h - 1)
                ins.then_inc(s_l, 1)
                if reload:
                    act.wait_ge(s_read, it * (nh - 1) + nh - 1)
                    fi_in(it + 1, nh - 2)
                    act.wait_ge(s_l, it * NB + NB)
                    fi_in(it + 1, nh - 1)

            def exp(it, t, k):
                n = it * NB + t * TJ + k
                act.wait_ge(s_t, n * NCH + NCH + 2)
                flat = w[k].rearrange("p h n -> p (h n)")
                act.activation(flat, flat, ACT.Exp).then_inc(s_e, 1)

            def turn(it, t):
                for k in range(TJ):
                    if k < 2:
                        relus(it, t, k + 2)
                    else:
                        relus(it, t + 1, k - 2)
                    exp(it, t if k + 1 < TJ else t + 1, (k + 1) % TJ)

            def evacuate(it):
                act.wait_ge(s_acc, it + 1)
                for c in range(2):
                    act.copy(ot[:, c, :], ps[:, OUT + c, :]).then_inc(s_ev, 1)

            def tile(it, more):
                with act.Fori(0, NT - 1) as t:
                    turn(it, t)
                relus(it, NT - 1, 2)
                exp(it, NT - 1, 1)
                relus(it, NT - 1, 3, reload=more)
                exp(it, NT - 1, 2)
                exp(it, NT - 1, 3)
                if more:
                    relus(it + 1, 0, 0, new=True)
                    relus(it + 1, 0, 1)
                evacuate(it)
                if more:
                    exp(it + 1, 0, 0)

            for h in range(nh):
                fi_in(0, h)
            relus(0, 0, 0, new=True)
            relus(0, 0, 1)
            exp(0, 0, 0)
            with act.Fori(0, NIT2 - 1) as it:
                tile(it, True)
            tile(NIT2 - 1, False)

        @block.vector
        def _(dve):
            dve.sem_inc(s_t, 2)
            dve.sem_inc(s_post, 1)
            dve.wait_ge(s_c, 16 * (2 * NF + 4))
            dve.tensor_scalar(gwr[:], gwr[:], gate[:, 0:1], 2.0, ALU.mult, ALU.mult).then_inc(s_copy, 1)
            dve.wait_ge(s_copy, 1)
            c0 = coef[0:KD, 0, :].rearrange("p (h n) -> p h n", n=R)
            dve.tensor_tensor(c0, c0, gwr[:].unsqueeze(2).broadcast_to([KD, nh, R]), ALU.mult).then_inc(s_copy, 1)
            dve.wait_ge(s_copy, 2)
            dve.tensor_copy(coef[0:KD, 1:G2, :], coef[0:KD, 0:1, :].broadcast_to([KD, G2 - 1, P])).then_inc(s_c2, 1)

            def differences(it, t, e, part):
                dp = it * (NB // 2) + t * (TJ // 2) + e
                if part == 0:
                    dve.wait_ge(s_b, dp * (2 * NCH) + 2 * NCH)
                for g in range(part * PG, (part + 1) * PG):
                    ins = dve.tensor_scalar(diff[0:KD, e, g, :], cj[:, bass.ds(t * (2 * JP) + e * JP, JP)],
                                            ci[:, bass.ds(it * G2 + g, 1)], 0.0, ALU.subtract, ALU.max)
                ins.then_inc(s_d, 1)

            def add(it, t, k, chunks, more=True):
                n = it * NB + t * TJ + k
                dve.wait_ge(s_l, n + 1)
                for c in chunks:
                    part = (k % 2) * NCH + c
                    if k < 2:
                        differences(it, t, 1, part)
                    elif isinstance(t, int) and t == NT - 1:
                        if more:
                            differences(it + 1, 0, 0, part)
                    else:
                        differences(it, t + 1, 0, part)
                    dve.wait_ge(s_b, n * NCH + c + 1 + 16)
                    l = w[k][:, :, c * P:(c + 1) * P].rearrange("p h (g i) -> p g h i", i=R)
                    bank = 2 * (c % 2)
                    b = ps[:, bank:bank + 2, :].rearrange("p a (g h i) -> p (a g) h i", h=nh, i=R)
                    dve.tensor_tensor(l, b, l, ALU.add).then_inc(s_t, 1)

            every = range(NCH)
            for part in range(PARTS):
                differences(0, 0, 0, part)
            add(0, 0, 0, every)
            add(0, 0, 1, every)
            links = 5

            def tile(it, more):
                for k in range(2, TJ):
                    add(it, 0, k, every)
                with dve.Fori(1, NT - 1) as t:
                    for k in range(TJ):
                        add(it, t, k, every)
                for k in range(TJ):
                    add(it, NT - 1, k, every, more)
                if more:
                    add(it + 1, 0, 0, every)
                dve.wait_ge(s_acc, it + 1)
                for c in range(2, 4):
                    dve.tensor_copy(ot[:, c, :], ps[:, OUT + c, :]).then_inc(s_ev, 1)
                if more:
                    add(it + 1, 0, 1, every[:2])
                count = [0]

                def link(ins):
                    count[0] += 1
                    ins.then_inc(s_link, 1)
                    dve.wait_ge(s_link, it * links + count[0])
                turned = ps[:, OUT:OUT + IB2, :].rearrange("p b (h m) -> p b h m", m=64)
                wide = [P, IB2, nh, d]
                a4 = att[:].rearrange("p b (h d) -> p b h d", h=nh)
                m4 = mean_v[:].rearrange("p (h d) -> p h d", h=nh).unsqueeze(1).broadcast_to(wide)
                dve.wait_ge(s_ot, it + 1)
                link(dve.tensor_copy(den[:, 0], turned[:, :, :, d]))
                link(dve.tensor_scalar(den[:, 1], den[:, 0], 0.0, None, ALU.is_equal))
                link(dve.tensor_tensor(den[:, 2], den[:, 0], den[:, 1], ALU.add))
                link(dve.reciprocal(den[:, 3], den[:, 2]))
                dve.tensor_tensor(a4, turned[:, :, :, 0:d], den[:, 3].unsqueeze(3).broadcast_to(wide),
                                  ALU.mult).then_inc(s_post, 1)
                if more:
                    add(it + 1, 0, 1, every[2:])
                dve.wait_ge(s_post, it + 2)
                dve.wait_ge(s_xi, it * 16 + 16)
                dve.tensor_tensor(xr[:], xr[:], att[:], ALU.add).then_inc(s_xa, 1)
                dve.wait_ge(s_xa, it * 2 + 1)
                link(dve.tensor_tensor(a4, m4, den[:, 1].unsqueeze(3).broadcast_to(wide), ALU.mult))
                dve.tensor_tensor(xr[:], xr[:], att[:], ALU.add).then_inc(s_xa, 1)

            with dve.Fori(0, NIT2 - 1) as it:
                tile(it, True)
            tile(NIT2 - 1, False)

        @block.tensor
        def _(pe):
            pe.sem_inc(s_b, 16)
            pe.sem_inc(s_pv, TJ)
            pe.wait_ge(s_c2, 1)
            pe.wait_ge(s_one, 16)

            def contract(k, pairs):
                for p in pairs:
                    for e in range(2):
                        h = 2 * p + e
                        ins = pe.matmul(ps[64 * e:64 * e + d + 1, OUT + p, :], aux[:, k, (d + 1) * h:(d + 1) * (h + 1)],
                                        w[k][:, h, :], start=False, stop=False, skip_group_check=True)
                return ins

            def bias_chunk(it, t, k, c):
                n = it * NB + t * TJ + k
                e = k // 2
                if k % 2 == 0 and c == 0:
                    dp = it * (NB // 2) + t * (TJ // 2) + e
                    pe.wait_ge(s_d, dp * PARTS + PARTS)
                if c == 0:
                    pe.wait_ge(s_m[e], (it * NT + t) * 48 + 48)
                pe.wait_ge(s_t, n * NCH + c + 1)
                for g in range(CG):
                    col = (g % 4) * P
                    ins = pe.matmul(ps[:, 2 * (c % 2) + g // 4, col:col + P],
                                    diff[0:KM, e, c * CG + g, (k % 2) * P:(k % 2 + 1) * P],
                                    coef[:, c * CG + g, :], start=True, stop=True)
                ins.then_inc(s_b, 1)

            def step(it, t, k, ahead=True):
                for c in range(NCH):
                    if ahead:
                        bias_chunk(it, t if k < 2 else t + 1, (k + 2) % TJ, c)
                    if c == 0:
                        pe.wait_ge(s_e, it * NB + t * TJ + k + 1)
                    ins = contract(k, [c])
                ins.then_inc(s_pv, 1)

            def clear():
                for c in range(4):
                    pe.matmul(ps[:, OUT + c, :], zeros[:, 0:P], zeros[:], start=True, stop=False, skip_group_check=True)

            def tile(it, more):
                with pe.Fori(0, NT - 1) as t:
                    for k in range(TJ):
                        step(it, t, k)
                for k in range(2):
                    step(it, NT - 1, k)
                step(it, NT - 1, 2, False)
                if more:
                    pe.wait_ge(s_r, it * 16 + 32)
                    for c in range(NCH):
                        bias_chunk(it + 1, 0, 0, c)
                step(it, NT - 1, 3, False)
                for c in range(4):
                    ins = pe.matmul(ps[:, OUT + c, :], zeros[:, 0:P], zeros[:], start=False, stop=True, skip_group_check=True)
                ins.then_inc(s_acc, 1)
                if more:
                    bias_chunk(it + 1, 0, 1, 0)
                    bias_chunk(it + 1, 0, 1, 1)
                pe.wait_ge(s_ev, it * 4 + 4)
                for b in range(IB2):
                    for p in range(4):
                        ins = pe.transpose(ps[:, OUT + b, p * P:(p + 1) * P], ot[:, p, b * P:(b + 1) * P], ident[:])
                ins.then_inc(s_ot, 1)
                if more:
                    bias_chunk(it + 1, 0, 1, 2)
                    bias_chunk(it + 1, 0, 1, 3)
                    pe.wait_ge(s_post, it + 2)
                    clear()

            pe.wait_ge(s_r, 16)
            for k in range(2):
                for c in range(NCH):
                    bias_chunk(0, 0, k, c)
            clear()
            with pe.Fori(0, NIT2 - 1) as it:
                tile(it, True)
            tile(NIT2 - 1, False)


def build(nc, a, out, layers):
    with ExitStack() as ctx:
        def sb(name, shape, dt=F32):
            return ctx.enter_context(nc.sbuf_tensor(name, shape, dt))

        def dram(name, shape, dt=F32):
            return nc.dram_tensor(name, shape, dt, kind="Internal").ap()

        def phase(f, prefix, *args):
            made = []

            def sem(name):
                made.append(nc.alloc_semaphore(name=f"{prefix}_{name}"))
                return made[-1]
            f(nc, sem, ps, keep, *args)
            nc.clear_and_free_semaphores(made)
            nc.all_engine_barrier()
        ps = ctx.enter_context(nc.psum_tensor("ps", [P, 8, BANK], F32))
        keep = {
            "x": sb("x", [P, NB, F]), "mean_v": sb("mean_v", [P, F]), "ident": sb("ident", [P, P]),
            "ones": sb("ones", [P, P]), "zeros": sb("zeros", [P, BANK], BF16),
            "j_part": sb("j_part", [P, 3, NB, NH2]), "one_cols": sb("one_cols", [P, 32]),
        }
        x = keep["x"]
        s_x = [ctx.enter_context(nc.semaphore(f"x_in{k}")) for k in range(4)]
        s_i, s_c = ctx.enter_context(nc.semaphore("ident_in")), ctx.enter_context(nc.semaphore("constants"))
        with nc.Block() as block:
            @block.sync
            def _(sp):
                for k in range(4):
                    part = slice(k * NB // 4, (k + 1) * NB // 4)
                    sp.dma_start(x[:, part], a["x"].rearrange("(b p) f -> p b f", p=P)[:, part]).then_inc(s_x[k], 16)
                sp.dma_start(keep["ident"][:], a["ident"]).then_inc(s_i, 16)
                sp.wait_ge(s_i, 16)

            @block.vector
            def _(dve):
                dve.memset(keep["ones"][:], 1.0 / N).then_inc(s_c, 1)
                dve.memset(keep["zeros"][:], 0.0).then_inc(s_c, 1)
                dve.memset(keep["one_cols"][:], 1.0).then_inc(s_c, 1)
                dve.wait_ge(s_c, 3)
        w1a, w1b = a["W1"], a["W2"]
        less_1 = dram("less_1", [N, N])
        if "0" in layers:
            l0 = dict(name="l0", nh=1, d=F, src=x, norm=True, loads=s_x, w=a["eye"], jvec=a["a0"][F:2 * F, 0], ivec=a["a0"][0:F, 0],
                      aux=dram("aux0", [NB, P, F]), irow=dram("irow0", [NB, 1, P]), elu=False, mean=True)
            phase(prepare, "p0", l0)
            phase(attend, "l0", l0, a["adj_t"])
        if "1" in layers:
            with nc.sbuf_tensor("h1", [P, NB, F], F32) as h1:
                for name, src, w, av, dst in (("l1a", x, w1a, a["a1"], h1), ("l1b", h1, w1b, a["a2"], None)):
                    l1 = dict(name=name, nh=4, d=64, src=src, norm=dst is not None, w=w, jvec=av[1], ivec=av[0],
                              aux=dram("aux" + name, [NB, P, F]), irow=dram("irow" + name, [NB, 4, P]),
                              elu=True, mean=True, dst=dst,
                              mask={"adj": a["adj"], "less_1": less_1, "first": 0 if dst is not None else NB // 2})
                    phase(prepare, "p" + name, l1)
                    phase(attend, name, l1, a["adj_t"])
        if "2" in layers:
            l2 = dict(name="l2", nh=8, d=32, src=x, norm=True, w=a["w2"], jvec=a["ar2"], ivec=a["al2"],
                      aux=dram("aux2", [NB, P, F + 8]), irow=dram("irow2", [NB, 8, P]), elu=False, mean=True,
                      pair={"curv": a["curv"], "wc": a["wc"], "gate": a["gate"], "brow": dram("brow2", [NB, 8, P]),
                            "curv_t": a["curv_t"], "wc_t": a["wc_t"], "curv_g": a["curv_g"], "same_i": a["same_i"], "one_row": a["one_row"],
                            "krow": dram("krow2", [NB, 8, P]), "x_rows": dram("x_rows", [N, F]),
                            "less_1": less_1, "shifts": dram("shifts2", [NIT2, IT2 * NH2])})
            phase(prepare, "p2", l2)
            phase(attend_pairwise, "l2", l2)
        if "3" in layers:
            l3 = dict(name="l3", nh=4, d=64, src=x, norm=True, w=a["w3"], jvec=a["u3"], ivec=a["v3"],
                      aux=dram("aux3", [NB, P, F]), irow=dram("irow3", [NB, 4, P]),
                      elu=False, mean=False, nonzero=True, proj={"w": a["pw3"], "bias": [a["b3"], a["pb3"]]})
            phase(prepare, "p3", l3)
            phase(attend, "l3", l3, a["adj_t"])
        s_o = ctx.enter_context(nc.semaphore("out_written"))
        with nc.Block() as block:
            @block.sync
            def _(sp):
                sp.dma_start(out.rearrange("(b p) f -> p b f", p=P), x[:]).then_inc(s_o, 16)
                sp.wait_ge(s_o, 16)


LAYERS = "0123"


def kernel(**inputs):
    import numpy as _np
    import concourse.bacc as _bacc
    from concourse import mybir as _mybir
    from concourse.bass_utils import run_bass_kernel_spmd as _run

    i = {k: _np.asarray(v) for k, v in inputs.items()}
    heads = lambda w: w.transpose(1, 0, 2).reshape(F, F)
    halves = lambda v: v.reshape(4, 2, 64).transpose(1, 0, 2).reshape(2, F)
    same_i = _np.zeros((KM - 1, NH2, R), _np.float32)
    for r in range(R):
        same_i[r:KD:R, :, r] = 1.0
        same_i[KD + r, :, r] = BIG
    for h in range(NH2):
        same_i[KD + R + h, h, :] = 1.0
    curv = i["L2_gnn_curv_feats"]
    put = {
        "adj": i["adj"], "w2": i["L2_gnn_W"].T, "al2": i["L2_gnn_a_l"].reshape(F), "ar2": i["L2_gnn_a_r"].reshape(F),
        "curv": curv, "curv_t": curv.T, "curv_g": curv.reshape(GN, R, NF).transpose(2, 1, 0).reshape(KD, GN),
        "wc": i["L2_gnn_Wc"], "wc_t": i["L2_gnn_Wc"].T, "gate": i["L2_gnn_gate"].reshape(1),
        "same_i": same_i.reshape(KM - 1, P), "one_row": _np.ones((2 * G2, JP), _np.float32),
        "x": i["x"], "adj_t": i["adj"].T, "a0": i["L0_gnn_a"],
        "W1": heads(i["L1_gnn_W1"]), "a1": halves(i["L1_gnn_a1"]),
        "W2": heads(i["L1_gnn_W2"]), "a2": halves(i["L1_gnn_a2"]),
        "w3": i["L3_gnn_weight"], "u3": i["L3_gnn_weight_u"].reshape(F), "v3": i["L3_gnn_weight_v"].reshape(F),
        "b3": i["L3_gnn_bias"].reshape(F), "pb3": i["L3_gnn_proj_b"], "pw3": i["L3_gnn_proj_w"].T,
        "ident": _np.eye(P, dtype=_np.float32), "eye": _np.eye(F, dtype=_np.float32),
    }
    nc = _bacc.Bacc("TRN2", target_bir_lowering=False, num_devices=1)
    arrays, aps = {}, {}
    for name, v in put.items():
        v = _np.ascontiguousarray(v)
        arrays[name + "_dram"] = v
        aps[name] = nc.dram_tensor(name + "_dram", v.shape, _mybir.dt.from_np(v.dtype), kind="ExternalInput").ap()
    o = nc.dram_tensor("out_dram", (N, F), F32, kind="ExternalOutput").ap()
    build(nc, aps, o, LAYERS)
    r = _run(nc, [arrays], core_ids=[0])
    return r.results[0]["out_dram"]
```
